# Optimizing a Trainium2 kernel written in Bass

```python
import numpy as np
import jax
import jax.numpy as jnp

def _softmax(x, axis=-1):
    return jax.nn.softmax(x, axis=axis)

def _gelu(x):
    return jax.nn.gelu(x, approximate=True)

def _silu(x):
    return jax.nn.silu(x)

def _sigmoid(x):
    return jax.nn.sigmoid(x)

def _layernorm(x, axis=-1, eps=1e-05):
    m = jnp.mean(x, axis=axis, keepdims=True)
    v = jnp.var(x, axis=axis, keepdims=True)
    return (x - m) / jnp.sqrt(v + eps)

def _scatter_add(tgt, idx, src, axis=0):
    return tgt.at[idx].add(src)

def _segment_sum(src, seg, n):
    return jax.ops.segment_sum(src, seg, n)
kernel_name = 'mk_sandwich_d1_jaxref_r8_7df789'

def setup_inputs(seed: int=0):
    np.random.seed(seed)
    _w = jnp.asarray

    def _L0_attn_setup():
        import jax, jax.numpy as jnp
        import numpy as np
        B, L, E, D, H = (2, 256, 128, 128, 8)

        def _ln(x, g, b, eps=1e-05):
            m = jnp.mean(x, axis=-1, keepdims=True)
            v = jnp.mean((x - m) ** 2, axis=-1, keepdims=True)
            return (x - m) * jax.lax.rsqrt(v + eps) * g + b
        key = jax.random.key(seed)
        ks = jax.random.split(key, 10)
        s = 0.02

        def n(k, shape):
            return jax.random.normal(k, shape, jnp.float32) * s
        return {'emb': jax.random.normal(ks[0], (B, L, E), jnp.float32), 'Wa_w': n(ks[1], (H, D, E)), 'Wa_b': jnp.zeros((H, D), jnp.float32), 'Wb_w': n(ks[2], (H, D, E)), 'Wb_b': jnp.zeros((H, D), jnp.float32), 'C_w': n(ks[3], (H, D, D)), 'C_b': jnp.zeros((H, D), jnp.float32), 'D_w': n(ks[4], (D, E)), 'D_b': jnp.zeros((D,), jnp.float32), 'Wout_w': n(ks[5], (E, D)), 'Wout_b': jnp.zeros((E,), jnp.float32), 'hn_g': jnp.ones((H, D), jnp.float32), 'hn_b': jnp.zeros((H, D), jnp.float32), 'head_w': jnp.ones((H,), jnp.float32), 'ffn1_w': n(ks[6], (4 * E, E)), 'ffn1_b': jnp.zeros((4 * E,), jnp.float32), 'ffn2_w': n(ks[7], (E, 4 * E)), 'ffn2_b': jnp.zeros((E,), jnp.float32), 'proj_w': n(ks[8], (E, E)), 'proj_b': jnp.zeros((E,), jnp.float32), 'norm_g': jnp.ones((E,), jnp.float32), 'norm_b': jnp.zeros((E,), jnp.float32)}
    _L0_attn_in = _L0_attn_setup()

    def _L0_ffn_setup():
        import jax, jax.numpy as jnp
        import numpy as np
        import math
        N_EMBD = 128
        HIDDEN = 4 * N_EMBD
        N_EXPERTS = 8
        TOP_K = 2
        B, T = (4, 256)

        def new_gelu(x):
            c = math.sqrt(2.0 / math.pi)
            return 0.5 * x * (1.0 + jnp.tanh(c * (x + 0.044715 * x * x * x)))

        def _moe_forward(x, Wfc_s, bfc_s, Wproj_s, bproj_s, Wr, Wfc, bfc, Wproj, bproj):
            Bb, Tt, C = x.shape
            xf = x.reshape(Bb * Tt, C)
            N = Bb * Tt
            shared = new_gelu(xf @ Wfc_s + bfc_s) @ Wproj_s + bproj_s
            logits = xf @ Wr
            probs = jax.nn.softmax(logits, axis=-1)
            topk_p, topk_i = jax.lax.top_k(probs, TOP_K)
            topk_p = topk_p / jnp.sum(topk_p, axis=-1, keepdims=True)
            gate = jnp.zeros((N, N_EXPERTS), dtype=xf.dtype)
            gate = gate.at[jnp.arange(N)[:, None], topk_i].add(topk_p)
            routed = jnp.zeros_like(xf)
            for e in range(N_EXPERTS):
                h = new_gelu(xf @ Wfc[e] + bfc[e]) @ Wproj[e] + bproj[e]
                routed = routed + h * gate[:, e:e + 1]
            return (shared + routed).reshape(Bb, Tt, C)
        key = jax.random.key(seed)
        ks = jax.random.split(key, 10)
        s = 0.02
        return {'x': jax.random.normal(ks[0], (B, T, N_EMBD), dtype=jnp.float32), 'Wfc_s': jax.random.normal(ks[1], (N_EMBD, HIDDEN), dtype=jnp.float32) * s, 'bfc_s': jnp.zeros((HIDDEN,), dtype=jnp.float32), 'Wproj_s': jax.random.normal(ks[2], (HIDDEN, N_EMBD), dtype=jnp.float32) * s, 'bproj_s': jnp.zeros((N_EMBD,), dtype=jnp.float32), 'Wr': jax.random.normal(ks[3], (N_EMBD, N_EXPERTS), dtype=jnp.float32) * s, 'Wfc': jax.random.normal(ks[4], (N_EXPERTS, N_EMBD, HIDDEN), dtype=jnp.float32) * s, 'bfc': jnp.zeros((N_EXPERTS, HIDDEN), dtype=jnp.float32), 'Wproj': jax.random.normal(ks[5], (N_EXPERTS, HIDDEN, N_EMBD), dtype=jnp.float32) * s, 'bproj': jnp.zeros((N_EXPERTS, N_EMBD), dtype=jnp.float32)}
    _L0_ffn_in = _L0_ffn_setup()
    _d = {'L0_attn_emb': _L0_attn_in['emb'], 'L0_attn_Wa_w': _L0_attn_in['Wa_w'], 'L0_attn_Wa_b': _L0_attn_in['Wa_b'], 'L0_attn_Wb_w': _L0_attn_in['Wb_w'], 'L0_attn_Wb_b': _L0_attn_in['Wb_b'], 'L0_attn_C_w': _L0_attn_in['C_w'], 'L0_attn_C_b': _L0_attn_in['C_b'], 'L0_attn_D_w': _L0_attn_in['D_w'], 'L0_attn_D_b': _L0_attn_in['D_b'], 'L0_attn_Wout_w': _L0_attn_in['Wout_w'], 'L0_attn_Wout_b': _L0_attn_in['Wout_b'], 'L0_attn_hn_g': _L0_attn_in['hn_g'], 'L0_attn_hn_b': _L0_attn_in['hn_b'], 'L0_attn_head_w': _L0_attn_in['head_w'], 'L0_attn_ffn1_w': _L0_attn_in['ffn1_w'], 'L0_attn_ffn1_b': _L0_attn_in['ffn1_b'], 'L0_attn_ffn2_w': _L0_attn_in['ffn2_w'], 'L0_attn_ffn2_b': _L0_attn_in['ffn2_b'], 'L0_attn_proj_w': _L0_attn_in['proj_w'], 'L0_attn_proj_b': _L0_attn_in['proj_b'], 'L0_attn_norm_g': _L0_attn_in['norm_g'], 'L0_attn_norm_b': _L0_attn_in['norm_b'], 'L0_ffn_Wfc_s': _L0_ffn_in['Wfc_s'], 'L0_ffn_bfc_s': _L0_ffn_in['bfc_s'], 'L0_ffn_Wproj_s': _L0_ffn_in['Wproj_s'], 'L0_ffn_bproj_s': _L0_ffn_in['bproj_s'], 'L0_ffn_Wr': _L0_ffn_in['Wr'], 'L0_ffn_Wfc': _L0_ffn_in['Wfc'], 'L0_ffn_bfc': _L0_ffn_in['bfc'], 'L0_ffn_Wproj': _L0_ffn_in['Wproj'], 'L0_ffn_bproj': _L0_ffn_in['bproj']}
    _x0 = _d['L0_attn_emb']
    _d['L0_attn_emb'] = jax.random.normal(jax.random.fold_in(jax.random.key(seed), 1), (4, 512, 128), dtype=_x0.dtype)
    del _x0
    return _d

def reference(L0_attn_emb, L0_attn_Wa_w, L0_attn_Wa_b, L0_attn_Wb_w, L0_attn_Wb_b, L0_attn_C_w, L0_attn_C_b, L0_attn_D_w, L0_attn_D_b, L0_attn_Wout_w, L0_attn_Wout_b, L0_attn_hn_g, L0_attn_hn_b, L0_attn_head_w, L0_attn_ffn1_w, L0_attn_ffn1_b, L0_attn_ffn2_w, L0_attn_ffn2_b, L0_attn_proj_w, L0_attn_proj_b, L0_attn_norm_g, L0_attn_norm_b, L0_ffn_Wfc_s, L0_ffn_bfc_s, L0_ffn_Wproj_s, L0_ffn_bproj_s, L0_ffn_Wr, L0_ffn_Wfc, L0_ffn_bfc, L0_ffn_Wproj, L0_ffn_bproj):

    def _L0_attn_ref(emb, Wa_w, Wa_b, Wb_w, Wb_b, C_w, C_b, D_w, D_b, Wout_w, Wout_b, hn_g, hn_b, head_w, ffn1_w, ffn1_b, ffn2_w, ffn2_b, proj_w, proj_b, norm_g, norm_b):
        import jax, jax.numpy as jnp
        import numpy as np
        B, L, E, D, H = (2, 256, 128, 128, 8)

        def _ln(x, g, b, eps=1e-05):
            m = jnp.mean(x, axis=-1, keepdims=True)
            v = jnp.mean((x - m) ** 2, axis=-1, keepdims=True)
            return (x - m) * jax.lax.rsqrt(v + eps) * g + b
        nH = head_w.shape[0]
        a = jnp.tanh(jnp.einsum('ble,hde->blhd', emb, Wa_w) + Wa_b)
        bg = jnp.einsum('ble,hde->blhd', emb, Wb_w) + Wb_b
        aT = jnp.moveaxis(a, 1, 0)
        bT = jnp.moveaxis(bg, 1, 0)

        def step(h, ab):
            at, bt = ab
            h = at * h + bt
            return (h, h)
        h0 = jnp.zeros_like(aT[0])
        _, hs = jax.lax.scan(step, h0, (aT, bT))
        hs = jnp.moveaxis(hs, 0, 1)
        Dx = emb @ D_w.T + D_b
        out = (jnp.einsum('blhd,hkd->blhk', hs, C_w) + C_b) * Dx[:, :, None, :]
        out = _ln(out, hn_g, hn_b)
        sum_heads = (Dx + jnp.einsum('h,blhd->bld', head_w, out)) / nH
        z = sum_heads @ Wout_w.T + Wout_b
        u = z + _ln(z, norm_g, norm_b)
        ffn = jax.nn.gelu(u @ ffn1_w.T + ffn1_b, approximate=False)
        h_out = u + (ffn @ ffn2_w.T + ffn2_b)
        return h_out @ proj_w.T + proj_b

    def _L0_ffn_ref(x, Wfc_s, bfc_s, Wproj_s, bproj_s, Wr, Wfc, bfc, Wproj, bproj):
        import jax, jax.numpy as jnp
        import numpy as np
        import math
        N_EMBD = 128
        HIDDEN = 4 * N_EMBD
        N_EXPERTS = 8
        TOP_K = 2
        B, T = (4, 256)

        def new_gelu(x):
            c = math.sqrt(2.0 / math.pi)
            return 0.5 * x * (1.0 + jnp.tanh(c * (x + 0.044715 * x * x * x)))

        def _moe_forward(x, Wfc_s, bfc_s, Wproj_s, bproj_s, Wr, Wfc, bfc, Wproj, bproj):
            Bb, Tt, C = x.shape
            xf = x.reshape(Bb * Tt, C)
            N = Bb * Tt
            shared = new_gelu(xf @ Wfc_s + bfc_s) @ Wproj_s + bproj_s
            logits = xf @ Wr
            probs = jax.nn.softmax(logits, axis=-1)
            topk_p, topk_i = jax.lax.top_k(probs, TOP_K)
            topk_p = topk_p / jnp.sum(topk_p, axis=-1, keepdims=True)
            gate = jnp.zeros((N, N_EXPERTS), dtype=xf.dtype)
            gate = gate.at[jnp.arange(N)[:, None], topk_i].add(topk_p)
            routed = jnp.zeros_like(xf)
            for e in range(N_EXPERTS):
                h = new_gelu(xf @ Wfc[e] + bfc[e]) @ Wproj[e] + bproj[e]
                routed = routed + h * gate[:, e:e + 1]
            return (shared + routed).reshape(Bb, Tt, C)
        return _moe_forward(x, Wfc_s, bfc_s, Wproj_s, bproj_s, Wr, Wfc, bfc, Wproj, bproj)
    x = L0_attn_emb
    x = x + _layernorm(_L0_attn_ref(_layernorm(x, axis=-1), L0_attn_Wa_w, L0_attn_Wa_b, L0_attn_Wb_w, L0_attn_Wb_b, L0_attn_C_w, L0_attn_C_b, L0_attn_D_w, L0_attn_D_b, L0_attn_Wout_w, L0_attn_Wout_b, L0_attn_hn_g, L0_attn_hn_b, L0_attn_head_w, L0_attn_ffn1_w, L0_attn_ffn1_b, L0_attn_ffn2_w, L0_attn_ffn2_b, L0_attn_proj_w, L0_attn_proj_b, L0_attn_norm_g, L0_attn_norm_b), axis=-1)
    x = x + _layernorm(_L0_ffn_ref(_layernorm(x, axis=-1), L0_ffn_Wfc_s, L0_ffn_bfc_s, L0_ffn_Wproj_s, L0_ffn_bproj_s, L0_ffn_Wr, L0_ffn_Wfc, L0_ffn_bfc, L0_ffn_Wproj, L0_ffn_bproj), axis=-1)
    return x

_drawn_inputs = setup_inputs


def setup_inputs(seed=0):
    import zlib

    import numpy as np

    out = dict(_drawn_inputs(seed))
    spreads = {'L0_attn_Wa_b': (0.0, 0.1),
     'L0_attn_Wb_b': (0.0, 0.1),
     'L0_attn_C_b': (0.0, 0.1),
     'L0_attn_D_b': (0.0, 0.1),
     'L0_attn_Wout_b': (0.0, 0.1),
     'L0_attn_hn_g': (1.0, 0.2),
     'L0_attn_hn_b': (0.0, 0.1),
     'L0_attn_head_w': (1.0, 0.2),
     'L0_attn_ffn1_b': (0.0, 0.1),
     'L0_attn_ffn2_b': (0.0, 0.1),
     'L0_attn_proj_b': (0.0, 0.1),
     'L0_attn_norm_g': (1.0, 0.2),
     'L0_attn_norm_b': (0.0, 0.1),
     'L0_ffn_bfc_s': (0.0, 0.1),
     'L0_ffn_bproj_s': (0.0, 0.1),
     'L0_ffn_bfc': (0.0, 0.1),
     'L0_ffn_bproj': (0.0, 0.1)}
    factors = {}
    for name, (base, spread) in spreads.items():
        noise = np.random.default_rng([zlib.crc32(name.encode()), seed]).standard_normal(out[name].shape)
        drawn = base * np.exp(spread * noise) if base else spread * noise
        out[name] = jnp.asarray(drawn.astype(out[name].dtype))
    for name, factor in factors.items():
        out[name] = (out[name] * factor).astype(out[name].dtype)
    return out
```

```python
from contextlib import ExitStack

import concourse.bass as bass
from concourse import mybir

P = 128
B, L, E = 4, 512, 128
T = L // P
H = 8
X = 8
F = 4
NE = X + 1
NH = NE * F
EPS = 1e-5

WA_B, WB_B, C_B, D_B, HN_B = 0, H, 2 * H, 3 * H, 3 * H + 1
F1_B = HN_B + H
F2_B = F1_B + F
FC_B = F2_B + 1
PR_B = FC_B + NH
NPAR = PR_B + NE

SR = 6 * H
C_ID, C_HM = 0, P
C_EM = C_HM + H
C_HI = C_EM + X
C_LO = C_HI + 1
C_Q = C_LO + 1
C_IO = C_Q + 1
NCON = C_IO + X

NATIVE_DOWN = 1


def is_split(j):
    return j < F - NATIVE_DOWN


def splits(i):
    return sum(is_split(k % F) for k in range(i + 1))


NSP = splits(NH - 1)

BLOCKS = [("d", 0, 0)] + [(n, h, 0) for h in range(H) for n in "ab"] + [("f1", j, 0) for j in range(F)]
NA = len(BLOCKS)
BLOCKS += [(n, e, j) for e in range(NE) for n in ("up", "dn") for j in range(F) if n == "up" or is_split(j)]
BLOCK_AT = {b: i for i, b in enumerate(BLOCKS)}
NATIVE = [("c", h, 0) for h in range(H)] + [("wout", 0, 0)] + [("f2", j, 0) for j in range(F)] + [("proj", 0, 0)]
NNA = len(NATIVE)
NATIVE += [("dn", e, j) for e in range(NE) for j in range(F) if not is_split(j)]
NATIVE_AT = {b: i for i, b in enumerate(NATIVE)}
GW = 4
GROUPS = [(s, min(s + GW, end)) for start, end in ((0, NA), (NA, len(BLOCKS))) for s in range(start, end, GW)]
NG = len(GROUPS)
NGA = -(-NA // GW)
RAW = 3
R = 3

HH = 2
HN = H // HH
LINKS_A, LINKS_O = 29, 3

SLOTS = NH + 2
ORDER = {i: [] for i in range(SLOTS + 1)}
PLACES = [(0, "x_stats"), (1, "x_norm"), (2, "x_turn"), (3, "dx")]
for _h in range(H + 2):
    if _h < H:
        PLACES += [(3 + _h, "gates", _h)]
    if 1 <= _h <= H:
        PLACES += [(3 + _h, "out", _h - 1)]
    if _h >= 2:
        PLACES += [(3 + _h, "turn", _h - 2)]
PLACES += [(8, "h_var", 0), (10, "h_pack", 0), (12, "h_var", 1), (15, "h_pack", 1), (16, "h_turn")]
PLACES += [(17 + _h // 2, "scale", _h) for _h in range(H)]
PLACES += [(22, "z"), (24, "u"), (25, "u_turn"),
           (26, "ffn_up", 0), (26, "ffn_up", 1), (27, "ffn_down", 0), (27, "ffn_up", 2),
           (28, "ffn_down", 1), (28, "ffn_up", 3), (29, "ffn_down", 2), (29, "ffn_down", 3), (29, "h_out"),
           (30, "proj"), (32, "attention"), (34, "x1_norm"), (35, "x1_turn"),
           (36, "route"), (37, "gate"), (38, "gate_turn")]
for _slot, *_step in PLACES:
    ORDER[_slot].append(_step)


def build(nc, emb, weights, native, params, rows, heads, head_w, consts, out):
    fp32, f32r, u32 = mybir.dt.float32, mybir.dt.float32r, mybir.dt.uint32
    ALU, ACT = mybir.AluOpType, mybir.ActivationFunctionType
    AX = mybir.AxisListType.X
    ctx = ExitStack()
    with ctx:
        def sb(name, shape, dt=fp32):
            return ctx.enter_context(nc.sbuf_tensor(name, shape, dt))

        def sem(name):
            return ctx.enter_context(nc.semaphore(name))

        w_raw = sb("w_raw", [P, RAW, GW * P])
        w_hi = sb("w_hi", [P, len(BLOCKS), P], f32r)
        w_lo = sb("w_lo", [P, len(BLOCKS), P], f32r)
        w_nat = sb("w_nat", [P, len(NATIVE), P])
        w_router = sb("w_router", [P, P])
        par = sb("par", [P, NPAR])
        row = sb("row", [P, 4, P])
        con = sb("con", [P, NCON])
        hrow = sb("hrow", [P, P + 1])
        hhi = sb("hhi", [P, P], f32r)
        hlo = sb("hlo", [P, P])
        hstack = sb("hstack", [P, P])
        hsel = sb("hsel", [P, H + 1, P], f32r)
        esel = sb("esel", [P, X, P], f32r)
        hw = sb("hw", [P, H])
        hb = sb("hb", [P, H])
        dx8_b = sb("dx8_b", [P, 1])
        mhalf = sb("mhalf", [P, T * H])

        x_tok = sb("x_tok", [P, T, E])
        tok = sb("tok", [P, 2, T, E])
        xT_hi = sb("xT_hi", [P, L], f32r)
        xT_lo = sb("xT_lo", [P, L], f32r)
        dx = sb("dx", [P, L])
        acc = sb("acc", [P, L])
        a_t = sb("a_t", [P, 2, L])
        b_t = sb("b_t", [P, L])
        o_t = sb("o_t", [P, H, L])
        st_a = sb("st_a", [P, T, 6])
        mv_a = sb("mv_a", [P, T, 2])
        ve_a = sb("ve_a", [P, T])
        rs_a = sb("rs_a", [P, T])
        st_h = sb("st_h", [P, T * H, 6])
        sm_h = sb("sm_h", [P, T * H])
        df_h = sb("df_h", [P, T * H])
        m2_h = sb("m2_h", [P, T * H])
        ve_h = sb("ve_h", [P, T * H])
        rs_h = sb("rs_h", [P, T * H])
        q_h = sb("q_h", [P, T * H])
        rq = sb("rq", [P, T, P])

        x1 = sb("x1", [P, T, E])
        x1_out = sb("x1_out", [P, T, E])
        tokb = sb("tokb", [P, T, E])
        res = sb("res", [P, T, E])
        x2_f = sb("x2_f", [P, L])
        x2_hi = sb("x2_hi", [P, L], f32r)
        x2_lo = sb("x2_lo", [P, L], f32r)
        y_acc = sb("y_acc", [P, L])
        y_e = sb("y_e", [P, L])
        g_t = sb("g_t", [P, R, L])
        g_hi = sb("g_hi", [P, R, L], f32r)
        g_lo = sb("g_lo", [P, R, L], f32r)
        st_b = sb("st_b", [P, T, 6])
        mv_b = sb("mv_b", [P, T, 2])
        ve_b = sb("ve_b", [P, T])
        rs_b = sb("rs_b", [P, T])
        lg = sb("lg", [P, T, X])
        top = sb("top", [P, T, 8])
        idx = sb("idx", [P, T, 8], u32)
        idf = sb("idf", [P, T, 8])
        gap = sb("gap", [P, T])
        th = sb("th", [P, T])
        gv = sb("gv", [P, 2, T])
        g1 = sb("g1", [P, T, X])
        g2 = sb("g2", [P, T, X])
        gate = sb("gate", [P, T, P])
        gT = sb("gT", [P, L], f32r)

        ps = [ctx.enter_context(nc.psum_tensor(f"ps{i}", [P, L], fp32)) for i in range(8)]
        p_hid, p_y, p_g = ps[0:2], ps[2], ps[3]
        p_a, p_b, p_c, p_t = ps[4:8]

        s_raw = [sem(f"s_raw{i}") for i in range(RAW)]
        s_con, s_nat, s_natb, s_zero, s_whi, s_wlo, s_chain, s_bias, s_setup = (
            sem(n) for n in ("s_con", "s_nat", "s_natb", "s_zero", "s_whi", "s_wlo", "s_chain", "s_bias", "s_setup"))
        x_in = sem("x_in")
        va = sem("va")
        var_a = sem("var_a")
        rstd_a = sem("rstd_a")
        var_h = sem("var_h")
        rstd_h = sem("rstd_h")
        xh = sem("xh")
        xt_mm = sem("xt_mm")
        xt_hi = sem("xt_hi")
        xt_lo = sem("xt_lo")
        dx_mm = sem("dx_mm")
        dx_sb = sem("dx_sb")
        a_mm = sem("a_mm")
        a_sb = sem("a_sb")
        b_mm = sem("b_mm")
        b_sb = sem("b_sb")
        scan = sem("scan")
        c_mm = sem("c_mm")
        o_sb = sem("o_sb")
        ot_mm = sem("ot_mm")
        o_bn = sem("o_bn")
        rq_sb = sem("rq_sb")
        rq_mm = sem("rq_mm")
        rt_sb = sem("rt_sb")
        rb_mm = sem("rb_mm")
        q_mm = sem("q_mm")
        scaled = sem("scaled")
        summed = sem("summed")
        z_mm = sem("z_mm")
        u_sb = sem("u_sb")
        ut_mm = sem("ut_mm")
        ut_sb = sem("ut_sb")
        ut_lo = sem("ut_lo")
        f_mm = sem("f_mm")
        f_sb = sem("f_sb")
        f_dn = sem("f_dn")
        ho_sb = sem("ho_sb")
        p_mm = sem("p_mm")
        att = sem("att")
        x1_sb = sem("x1_sb")
        x1_kept = sem("x1_kept")
        var_x = sem("var_x")
        rstd_x = sem("rstd_x")
        x2_tok = sem("x2_tok")
        x2_mm = sem("x2_mm")
        x2_h = sem("x2_h")
        x2_l = sem("x2_l")
        lg_mm = sem("lg_mm")
        gap_sb = sem("gap_sb")
        th_sb = sem("th_sb")
        gate_sb = sem("gate_sb")
        gt_mm = sem("gt_mm")
        gt_sb = sem("gt_sb")
        up_mm = sem("up_mm")
        h_sb = sem("h_sb")
        h_hi = sem("h_hi")
        h_lo = sem("h_lo")
        dn_mm = sem("dn_mm")
        y_sb = sem("y_sb")
        gb_mm = sem("gb_mm")
        gated = sem("gated")
        y_sum = sem("y_sum")
        yt_mm = sem("yt_mm")
        vo = sem("vo")
        var_o = sem("var_o")
        rstd_o = sem("rstd_o")
        out_sb = sem("out_sb")
        stored = sem("stored")
        res_free = sem("res_free")

        def ident():
            return con[:, C_ID:C_ID + P]

        def col(k):
            return par[:, k:k + 1]

        def tile(t):
            return slice(t * P, (t + 1) * P)

        def wait(eng, s, value):
            if not isinstance(value, int) or value > 0:
                eng.wait_ge(s, value)

        def chunks(eng, alone, beside, last):
            alone()
            with eng.Fori(0, B - 1) as c:
                beside(c, c + 1)
            last(B - 1)

        block = ctx.enter_context(nc.Block())

        @block.sync
        def _(sp):
            def load(c):
                wait(sp, x1_sb, c)
                sp.dma_start(x_tok[:, :, :],
                             emb[bass.ds(c * L, L), :].rearrange("(t p) e -> p t e", p=P)).then_inc(x_in, 16)

            def store(c):
                sp.wait_ge(out_sb, c + 1)
                sp.dma_start(out[bass.ds(c * L, L), :].rearrange("(t p) e -> p t e", p=P),
                             res[:, :, :]).then_inc(stored, 16)
                sp.wait_ge(stored, c * 16 + 16)
                sp.sem_inc(res_free, 1)

            load(0)
            sp.dma_start(con[:, :], consts).then_inc(s_con, 16)
            sp.dma_start(par[:, :], params).then_inc(s_con, 16)
            sp.sem_inc(res_free, 1)
            for g, (b0, b1) in enumerate(GROUPS):
                if g >= RAW:
                    sp.wait_ge(s_wlo, g - RAW + 1)
                sp.dma_start(w_raw[:, g % RAW, 0:(b1 - b0) * P],
                             weights[:, b0 * P:b1 * P]).then_inc(s_raw[g % RAW], 16)
                if g == RAW - 1:
                    sp.dma_start(hw[:, :], head_w.partition_broadcast(P)).then_inc(s_con, 16)
                    sp.dma_start(hrow[0:SR, :], heads).then_inc(s_con, 16)
                    sp.dma_start(w_nat[:, 0:NNA, :],
                                 native[:, 0:NNA * P].rearrange("p (n e) -> p n e", e=P)).then_inc(s_nat, 16)
                    sp.dma_start(row[:, :, :], rows.partition_broadcast(P)).then_inc(s_con, 16)
                if g == NGA:
                    sp.wait_ge(s_zero, 3)
                    sp.dma_start(w_router[:, 0:X],
                                 native[:, len(NATIVE) * P:len(NATIVE) * P + X]).then_inc(s_natb, 16)
                    sp.dma_start(w_nat[:, NNA:, :],
                                 native[:, NNA * P:len(NATIVE) * P].rearrange("p (n e) -> p n e", e=P)
                                 ).then_inc(s_natb, 16)
            with sp.Fori(0, B - 1) as c:
                load(c + 1)
                store(c)
            store(B - 1)
            sp.wait_ge(stored, B * 16)

        N_CON = 5 * 16

        @block.gpsimd
        def _(pool):
            nc.gpsimd.memset(mhalf[:, :], -0.5).then_inc(s_zero, 1)
            nc.gpsimd.memset(hstack[:, :], 0.0).then_inc(s_zero, 1)
            nc.gpsimd.memset(w_router[:, :], 0.0).then_inc(s_zero, 1)
            nc.gpsimd.memset(rq[:, :, :], 0.0).then_inc(s_zero, 1)
            nc.gpsimd.memset(gate[:, :, :], 0.0).then_inc(s_zero, 1)
            pool.wait_ge(s_zero, 5)

            def rstd(out_, var, var_ready, n, done):
                pool.wait_ge(var_ready, n)
                nc.gpsimd.tensor_tensor(out=out_, in0=var, in1=mhalf[:, 0:out_.shape[1]],
                                        op=ALU.pow).then_inc(done, 1)

            def a_norms(c):
                rstd(rs_a[:, :], ve_a[:, :], var_a, c * 3 + 1, rstd_a)
                for k in range(HH):
                    half = slice(k * T * HN, (k + 1) * T * HN)
                    rstd(rs_h[:, half], ve_h[:, half], var_h, c * HH + k + 1, rstd_h)
                rstd(rs_a[:, :], ve_a[:, :], var_a, c * 3 + 2, rstd_a)
                rstd(rs_a[:, :], ve_a[:, :], var_a, c * 3 + 3, rstd_a)
                rstd(rs_b[:, :], ve_b[:, :], var_x, c + 1, rstd_x)

            def keep(c):
                pool.wait_ge(x1_sb, c + 1)
                wait(pool, out_sb, c)
                nc.gpsimd.nop(nofuse=True)
                nc.gpsimd.tensor_copy(x1_out[:, :, :], x1[:, :, :]).then_inc(x1_kept, 1)

            def o_norm(c):
                rstd(rs_b[:, :], ve_b[:, :], var_o, c + 1, rstd_o)

            def alone():
                a_norms(0)
                keep(0)

            def beside(c, ca):
                a_norms(ca)
                o_norm(c)
                keep(ca)

            chunks(pool, alone, beside, o_norm)

        @block.tensor
        def _(pe):
            def mm3(dst, name, x_hi, x_lo, start=True, stop=True):
                w = BLOCK_AT[name]
                nc.tensor.matmul(dst, w_hi[:, w, :], x_hi, start=start, stop=False)
                nc.tensor.matmul(dst, w_lo[:, w, :], x_hi, start=False, stop=False)
                return nc.tensor.matmul(dst, w_hi[:, w, :], x_lo, start=False, stop=stop)

            def transposes(dst, src):
                for t in range(T):
                    last = nc.tensor.transpose(dst[:, tile(t)], src(t), ident())
                return last

            def x_turn(c):
                pe.wait_ge(xh, c + 1)
                transposes(p_a, lambda t: tok[:, 0, t, :]).then_inc(xt_mm, 1)

            def dx_product(c):
                pe.wait_ge(xt_lo, c + 1)
                mm3(p_c[:, :], ("d", 0, 0), xT_hi[:, :], xT_lo[:, :]).then_inc(dx_mm, 1)

            def gates(c, h):
                if h == 0:
                    if isinstance(c, int):
                        pe.wait_ge(s_wlo, 1)
                else:
                    pe.wait_ge(a_sb, c * H + h)
                if isinstance(c, int):
                    pe.wait_ge(s_wlo, BLOCK_AT["b", h, 0] // GW + 1)
                mm3(p_a[:, :], ("a", h, 0), xT_hi[:, :], xT_lo[:, :]).then_inc(a_mm, 1)
                if h > 0:
                    pe.wait_ge(b_sb, c * H + h)
                mm3(p_b[:, :], ("b", h, 0), xT_hi[:, :], xT_lo[:, :]).then_inc(b_mm, 1)

            def head_out(c, h):
                pe.wait_ge(scan, c * H + h + 1)
                if h == 0:
                    pe.wait_ge(dx_sb, c + 1)
                    if isinstance(c, int):
                        pe.wait_ge(s_nat, 16)
                else:
                    pe.wait_ge(o_sb, c * H + h)
                nc.tensor.matmul(p_c[:, :], w_nat[:, NATIVE_AT["c", h, 0], :], o_t[:, h, :],
                                 start=True, stop=True).then_inc(c_mm, 1)

            def turn(c, h):
                pe.wait_ge(o_sb, c * H + h + 1)
                if h > 0:
                    pe.wait_ge(o_bn, c * H + h)
                transposes(p_t, lambda t: o_t[:, h, tile(t)]).then_inc(ot_mm, 1)

            def h_turn(c):
                pe.wait_ge(rq_sb, c * HH + HH)
                transposes(p_t, lambda t: rq[:, t, :]).then_inc(rq_mm, 1)

            def scale(c, h):
                if h == 0:
                    pe.wait_ge(rt_sb, c + 1)
                    if isinstance(c, int):
                        pe.wait_ge(s_setup, 1)
                if h >= 2:
                    pe.wait_ge(scaled, c * H + h - 1)
                nc.tensor.matmul((p_a, p_b)[h % 2][:, :], hsel[:, h, :], xT_hi[:, :],
                                 start=True, stop=True).then_inc(rb_mm, 1)
                if h == 1:
                    nc.tensor.matmul(p_c[:, :], hsel[:, H, :], xT_hi[:, :], start=True, stop=True).then_inc(q_mm, 1)

            def z(c):
                pe.wait_ge(summed, c * (H + 1) + H + 1)
                for t in range(T):
                    last = nc.tensor.matmul(p_a[:, tile(t)], acc[:, tile(t)], w_nat[:, NATIVE_AT["wout", 0, 0], :],
                                            start=True, stop=True)
                last.then_inc(z_mm, 1)

            def u_turn(c):
                pe.wait_ge(u_sb, c + 1)
                transposes(p_b, lambda t: tok[:, 1, t, :]).then_inc(ut_mm, 1)

            def ffn_up(c, j):
                if j == 0:
                    pe.wait_ge(ut_lo, c + 1)
                    if isinstance(c, int):
                        pe.wait_ge(s_wlo, NGA)
                if j >= 2:
                    pe.wait_ge(f_sb, c * F + j - 1)
                mm3((p_a, p_c)[j % 2][:, :], ("f1", j, 0), xT_hi[:, :], xT_lo[:, :]).then_inc(f_mm, 1)

            def ffn_down(c, j):
                pe.wait_ge(f_sb, c * F + j + 1)
                nc.tensor.matmul(p_t[:, :], w_nat[:, NATIVE_AT["f2", j, 0], :], a_t[:, j % 2, :],
                                 start=(j == 0), stop=(j == F - 1)).then_inc(f_dn, 1)

            def proj(c):
                pe.wait_ge(ho_sb, c + 1)
                for t in range(T):
                    last = nc.tensor.matmul(p_b[:, tile(t)], dx[:, tile(t)], w_nat[:, NATIVE_AT["proj", 0, 0], :],
                                            start=True, stop=True)
                last.then_inc(p_mm, 1)

            def x1_turn(c):
                pe.wait_ge(x2_tok, c + 1)
                transposes(p_a, lambda t: tokb[:, t, :]).then_inc(x2_mm, 1)

            def route(c):
                pe.wait_ge(x2_h, c + 1)
                if isinstance(c, int):
                    pe.wait_ge(s_natb, 32)
                for t in range(T):
                    last = nc.tensor.matmul(p_c[:, tile(t)], x2_f[:, tile(t)], w_router[:, :], start=True, stop=True)
                last.then_inc(lg_mm, 1)

            def gate_turn(c):
                pe.wait_ge(gate_sb, c + 1)
                transposes(p_t, lambda t: gate[:, t, :]).then_inc(gt_mm, 1)

            STEPS = {"x_turn": x_turn, "dx": dx_product, "gates": gates, "out": head_out, "turn": turn,
                     "h_turn": h_turn, "scale": scale, "z": z, "u_turn": u_turn, "ffn_up": ffn_up,
                     "ffn_down": ffn_down, "proj": proj, "x1_turn": x1_turn, "route": route, "gate_turn": gate_turn}

            def b_up(c, i):
                if i == 0:
                    pe.wait_ge(x2_l, c + 1)
                if i >= 2:
                    pe.wait_ge(h_sb, c * NH + i - 1)
                mm3(p_hid[i % 2][:, :], ("up", i // F, i % F), x2_hi[:, :], x2_lo[:, :]).then_inc(up_mm, 1)

            def b_gate_bc(c, e):
                if e == 1:
                    pe.wait_ge(gt_sb, c + 1)
                else:
                    pe.wait_ge(gated, c * X + e - 1)
                nc.tensor.matmul(p_g[:, :], esel[:, e - 1, :], gT[:, :], start=True, stop=True).then_inc(gb_mm, 1)

            def b_down(c, i):
                e, j = i // F, i % F
                if j == 0 and e >= 1:
                    pe.wait_ge(y_sb, c * NE + e)
                first, last = j == 0, j == F - 1
                if is_split(j):
                    pe.wait_ge(h_lo, c * NSP + splits(i))
                    ins = mm3(p_y[:, :], ("dn", e, j), g_hi[:, i % R, :], g_lo[:, i % R, :], start=first, stop=last)
                else:
                    pe.wait_ge(h_sb, c * NH + i + 1)
                    ins = nc.tensor.matmul(p_y[:, :], w_nat[:, NATIVE_AT["dn", e, j], :], g_t[:, i % R, :],
                                           start=first, stop=last)
                ins.then_inc(dn_mm, 1)

            def b_out(c):
                pe.wait_ge(y_sum, c * X + X)
                transposes(p_g, lambda t: y_acc[:, tile(t)]).then_inc(yt_mm, 1)

            def body(c, ca):
                for i in range(SLOTS + 1):
                    if c is not None and i < NH:
                        b_up(c, i)
                    if c is not None and 2 <= i < SLOTS:
                        b_down(c, i - 2)
                        if (i - 2) % F == 2 and i - 2 >= F:
                            b_gate_bc(c, (i - 2) // F)
                    if ca is not None:
                        for name, *arg in ORDER[i]:
                            if name in STEPS:
                                STEPS[name](ca, *arg)
                if c is not None:
                    b_out(c)

            pe.wait_ge(s_con, 2 * 16)
            pe.wait_ge(s_zero, 5)
            chunks(pe, lambda: body(None, 0), body, lambda c: body(c, None))

        @block.scalar
        def _(act):
            def copy(dst, src):
                return nc.scalar.activation(dst, src, ACT.Copy)

            def split_weights(g):
                b0, b1 = GROUPS[g]
                act.wait_ge(s_raw[g % RAW], 16 * (g // RAW + 1))
                copy(w_hi[:, b0:b1, :], w_raw[:, g % RAW, 0:(b1 - b0) * P]
                     .rearrange("p (b n) -> p b n", n=P)).then_inc(s_whi, 1)

            def x_turn(c):
                act.wait_ge(xt_mm, c + 1)
                copy(xT_hi[:, :], p_a[:, :]).then_inc(xt_hi, 1)

            def dx_start(c):
                act.wait_ge(dx_mm, c + 1)
                nc.scalar.activation(dx[:, :], p_c[:, :], ACT.Identity, bias=col(D_B))
                if isinstance(c, int):
                    act.wait_ge(s_bias, 1)
                nc.scalar.activation(acc[:, :], p_c[:, :], ACT.Identity, bias=dx8_b[:, :],
                                     scale=1.0 / H).then_inc(dx_sb, 1)

            def gates(c, h):
                act.wait_ge(a_mm, c * H + h + 1)
                if h >= 2:
                    act.wait_ge(scan, c * H + h - 1)
                nc.scalar.activation(a_t[:, h % 2, :], p_a[:, :], ACT.Tanh, bias=col(WA_B + h)).then_inc(a_sb, 1)
                act.wait_ge(b_mm, c * H + h + 1)
                if h >= 1:
                    act.wait_ge(scan, c * H + h)
                nc.scalar.activation(b_t[:, :], p_b[:, :], ACT.Identity, bias=col(WB_B + h)).then_inc(b_sb, 1)

            def h_turn(c):
                act.wait_ge(rq_mm, c + 1)
                copy(xT_hi[:, :], p_t[:, :]).then_inc(rt_sb, 1)

            def u_turn(c):
                act.wait_ge(ut_mm, c + 1)
                copy(xT_hi[:, :], p_b[:, :])
                nc.scalar.activation(dx[:, :], p_b[:, :], ACT.Identity, bias=col(F2_B)).then_inc(ut_sb, 1)

            def ffn_up(c, j):
                act.wait_ge(f_mm, c * F + j + 1)
                if j >= 2:
                    act.wait_ge(f_dn, c * F + j - 1)
                nc.scalar.activation(a_t[:, j % 2, :], (p_a, p_c)[j % 2][:, :], ACT.Gelu,
                                     bias=col(F1_B + j)).then_inc(f_sb, 1)

            def x1_turn(c):
                act.wait_ge(x2_mm, c + 1)
                wait(act, up_mm, c * NH)
                copy(x2_hi[:, :], p_a[:, :])
                copy(x2_f[:, :], p_a[:, :]).then_inc(x2_h, 1)

            def gate(c):
                act.wait_ge(gap_sb, c + 1)
                nc.scalar.activation(th[:, :], gap[:, :], ACT.Tanh, scale=0.5).then_inc(th_sb, 1)

            def gate_turn(c):
                act.wait_ge(gt_mm, c + 1)
                copy(gT[:, :], p_t[:, :]).then_inc(gt_sb, 1)

            STEPS = {"x_turn": x_turn, "dx": dx_start, "gates": gates, "h_turn": h_turn, "u_turn": u_turn,
                     "ffn_up": ffn_up, "x1_turn": x1_turn, "gate": gate, "gate_turn": gate_turn}

            def b_gelu(c, i):
                act.wait_ge(up_mm, c * NH + i + 1)
                nc.scalar.activation(g_t[:, i % R, :], p_hid[i % 2][:, :], ACT.Gelu_apprx_tanh,
                                     bias=col(FC_B + i)).then_inc(h_sb, 1)

            def b_hi(c, i):
                act.wait_ge(h_sb, c * NH + i + 1)
                copy(g_hi[:, i % R, :], g_t[:, i % R, :]).then_inc(h_hi, 1)

            def b_y(c, e):
                act.wait_ge(dn_mm, c * NH + e * F + F)
                if e >= 2:
                    act.wait_ge(y_sum, c * X + e - 1)
                nc.scalar.activation((y_e if e else y_acc)[:, :], p_y[:, :], ACT.Identity,
                                     bias=col(PR_B + e)).then_inc(y_sb, 1)

            def body(c, ca):
                for i in range(SLOTS + 1):
                    if c is not None and i < NH:
                        b_gelu(c, i)
                        if is_split(i % F):
                            b_hi(c, i)
                    if c is not None and i % F == 1 and i > F:
                        b_y(c, i // F - 1)
                    if ca is not None:
                        for name, *arg in ORDER[i]:
                            if name in STEPS:
                                STEPS[name](ca, *arg)
                    if c is None and NGA + i < NG:
                        split_weights(NGA + i)

            for g in range(NGA):
                split_weights(g)
            act.wait_ge(s_con, 2 * 16)
            chunks(act, lambda: body(None, 0), body, lambda c: body(c, None))

        @block.vector
        def _(dve):
            def f(ap):
                return ap.bitcast(fp32)

            class Chain:

                def __init__(self, s, links):
                    self.s, self.links, self.k = s, links, 0

                def link(self, c, ins):
                    self.k += 1
                    ins.then_inc(self.s, 1)
                    dve.wait_ge(self.s, c * self.links + self.k)

                def end(self):
                    assert self.k == self.links, (self.k, self.links)
                    self.k = 0

            ch, cho = Chain(va, LINKS_A), Chain(vo, LINKS_O)

            def v_tt(dst, a, b, op):
                return nc.vector.tensor_tensor(out=dst, in0=a, in1=b, op=op)

            def v_ts(dst, a, s1, s2, op0, op1):
                return nc.vector.tensor_scalar(out=dst, in0=a, scalar1=s1, scalar2=s2, op0=op0, op1=op1)

            def split_weights(g):
                b0, b1 = GROUPS[g]
                dve.wait_ge(s_whi, g + 1)
                v_tt(w_lo[:, b0:b1, :], w_raw[:, g % RAW, 0:(b1 - b0) * P].rearrange("p (b n) -> p b n", n=P),
                     f(w_hi[:, b0:b1, :]), ALU.subtract).then_inc(s_wlo, 1)

            def selectors():
                setup = [0]

                def link(ins):
                    setup[0] += 1
                    ins.then_inc(s_chain, 1)
                    dve.wait_ge(s_chain, setup[0])

                dve.wait_ge(s_con, N_CON)
                dve.wait_ge(s_zero, 5)
                link(v_tt(hb[:, :], par[:, HN_B:HN_B + H], hw[:, :], ALU.mult))
                link(nc.vector.reduce_sum(dx8_b[:, :], hb[:, :], axis=AX))
                link(v_tt(dx8_b[:, :], dx8_b[:, :], col(D_B), ALU.add))
                v_ts(dx8_b[:, :], dx8_b[:, :], 1.0 / H, None, ALU.mult, ALU.bypass).then_inc(s_bias, 1)
                link(v_ts(hrow[0:SR, 0:P], hrow[0:SR, 0:P], hrow[0:SR, P:P + 1], 1.0 / H, ALU.mult, ALU.mult))
                link(nc.vector.tensor_copy(hhi[0:SR, :], hrow[0:SR, 0:P]))
                link(v_tt(hlo[0:SR, :], hrow[0:SR, 0:P], f(hhi[0:SR, :]), ALU.subtract))
                link(v_ts(hlo[0:SR, :], hlo[0:SR, :], con[0:SR, C_LO:C_LO + 1], None, ALU.mult, ALU.bypass))
                link(nc.vector.scalar_tensor_tensor(out=hstack[0:SR, :], in0=f(hhi[0:SR, :]),
                                                    scalar=con[0:SR, C_HI:C_HI + 1], in1=hlo[0:SR, :],
                                                    op0=ALU.mult, op1=ALU.add))
                for h in range(H):
                    v_ts(hsel[:, h, :], hstack[:, :], con[:, C_HM + h:C_HM + h + 1], None, ALU.mult, ALU.bypass)
                v_ts(hsel[:, H, :], hstack[:, :], con[:, C_Q:C_Q + 1], None, ALU.mult, ALU.bypass)
                nc.vector.tensor_copy(esel[:, :, :],
                                      con[:, C_EM:C_EM + X].unsqueeze(2).to_broadcast([P, X, P])).then_inc(s_setup, 1)

            def stats(c, chain, src, st, mv, ve, ready):
                for t in range(T):
                    ins = nc.vector.bn_stats(out=st[:, t, :], in_=src(t))
                chain.link(c, ins)
                nc.vector.nop(nofuse=True)
                for t in range(T):
                    ins = nc.vector.bn_aggr(out=mv[:, t, :], in_=st[:, t, :])
                chain.link(c, ins)
                nc.vector.tensor_scalar_add(ve[:, :], mv[:, :, 1], EPS).then_inc(ready, 1)

            def normalise(dst, src, mv, rs):
                for t in range(T):
                    ins = v_ts(dst(t), src(t), mv[:, t, 0:1], rs[:, t:t + 1], ALU.subtract, ALU.mult)
                return ins

            def spread(r):
                return row[:, r:r + 1, :].to_broadcast([P, T, P])

            def x_stats(c):
                dve.wait_ge(x_in, c * 16 + 16)
                stats(c, ch, lambda t: x_tok[:, t, :], st_a, mv_a, ve_a, var_a)

            def x_norm(c):
                dve.wait_ge(rstd_a, c * 3 + 1)
                normalise(lambda t: tok[:, 0, t, :], lambda t: x_tok[:, t, :], mv_a, rs_a).then_inc(xh, 1)

            def x_turn(c):
                dve.wait_ge(xt_hi, c + 1)
                v_tt(xT_lo[:, :], p_a[:, :], f(xT_hi[:, :]), ALU.subtract).then_inc(xt_lo, 1)

            def gates(c, h):
                dve.wait_ge(b_sb, c * H + h + 1)
                nc.vector.tensor_tensor_scan(out=o_t[:, h, :], data0=a_t[:, h % 2, :], data1=b_t[:, :],
                                             initial=0.0, op0=ALU.mult, op1=ALU.add).then_inc(scan, 1)

            def head_out(c, h):
                dve.wait_ge(c_mm, c * H + h + 1)
                nc.vector.scalar_tensor_tensor(out=o_t[:, h, :], in0=p_c[:, :], scalar=col(C_B + h), in1=dx[:, :],
                                               op0=ALU.add, op1=ALU.mult).then_inc(o_sb, 1)

            def turn(c, h):
                dve.wait_ge(ot_mm, c * H + h + 1)
                for t in range(T):
                    ins = nc.vector.bn_stats(out=st_h[:, (h // HN * T + t) * HN + h % HN, :], in_=p_t[:, tile(t)])
                ins.then_inc(o_bn, 1)

            def h_var(c, k):
                half = slice(k * T * HN, (k + 1) * T * HN)
                dve.wait_ge(o_bn, c * H + (k + 1) * HN)
                me, m2e, mo, m2o = (st_h[:, half, n] for n in (1, 2, 4, 5))
                v_tt(df_h[:, half], me, mo, ALU.subtract)
                v_tt(sm_h[:, half], me, mo, ALU.add)
                ch.link(c, v_tt(m2_h[:, half], m2e, m2o, ALU.add))
                ch.link(c, v_tt(df_h[:, half], df_h[:, half], df_h[:, half], ALU.mult))
                ch.link(c, v_ts(df_h[:, half], df_h[:, half], 0.25, EPS, ALU.mult, ALU.add))
                nc.vector.scalar_tensor_tensor(out=ve_h[:, half], in0=m2_h[:, half], scalar=1.0 / P,
                                               in1=df_h[:, half], op0=ALU.mult, op1=ALU.add).then_inc(var_h, 1)

            def h_pack(c, k):
                half = slice(k * T * HN, (k + 1) * T * HN)
                dve.wait_ge(rstd_h, c * HH + k + 1)
                r = rs_h[:, half].rearrange("p (t h) -> p t h", h=HN)
                q = q_h[:, half].rearrange("p (t h) -> p t h", h=HN)

                def part(n):
                    return rq[:, :, n * H + k * HN:n * H + (k + 1) * HN]

                nc.vector.tensor_copy(part(0).bitcast(f32r), r)
                nc.vector.tensor_copy(part(2).bitcast(f32r), r)
                ch.link(c, nc.vector.scalar_tensor_tensor(out=q_h[:, half], in0=sm_h[:, half], scalar=-0.5,
                                                          in1=rs_h[:, half], op0=ALU.mult, op1=ALU.mult))
                v_tt(part(1), r, part(0), ALU.subtract)
                nc.vector.tensor_copy(part(5).bitcast(f32r), q)
                ch.link(c, nc.vector.tensor_copy(part(3).bitcast(f32r), q))
                v_tt(part(4), q, part(3), ALU.subtract).then_inc(rq_sb, 1)

            def scale(c, h):
                dve.wait_ge(rb_mm, c * H + h + 1)
                v_tt(o_t[:, h, :], o_t[:, h, :], (p_a, p_b)[h % 2][:, :], ALU.mult).then_inc(scaled, 1)
                if h == 1:
                    dve.wait_ge(q_mm, c + 1)
                    v_tt(acc[:, :], acc[:, :], p_c[:, :], ALU.add).then_inc(summed, 1)
                if h >= 1:
                    add_head(c, h - 1)
                if h == H - 1:
                    add_head(c, h)

            def add_head(c, h):
                dve.wait_ge(scaled, c * H + h + 1)
                dve.wait_ge(summed, c * (H + 1) + h + 1)
                v_tt(acc[:, :], acc[:, :], o_t[:, h, :], ALU.add).then_inc(summed, 1)

            def z(c):
                dve.wait_ge(z_mm, c + 1)
                ch.link(c, v_tt(tok[:, 0, :, :], p_a[:, :].rearrange("p (t e) -> p t e", e=E), spread(0), ALU.add))
                stats(c, ch, lambda t: tok[:, 0, t, :], st_a, mv_a, ve_a, var_a)
                ch.link(c, v_tt(tok[:, 1, :, :], tok[:, 0, :, :], spread(2), ALU.add))
                for t in range(T):
                    ins = nc.vector.scalar_tensor_tensor(out=tok[:, 0, t, :], in0=tok[:, 0, t, :],
                                                         scalar=mv_a[:, t, 0:1], in1=row[:, 1, :],
                                                         op0=ALU.subtract, op1=ALU.mult)
                ch.link(c, ins)

            def u(c):
                dve.wait_ge(rstd_a, c * 3 + 2)
                for t in range(T):
                    ins = nc.vector.scalar_tensor_tensor(out=tok[:, 1, t, :], in0=tok[:, 0, t, :],
                                                         scalar=rs_a[:, t:t + 1], in1=tok[:, 1, t, :],
                                                         op0=ALU.mult, op1=ALU.add)
                ins.then_inc(u_sb, 1)

            def u_turn(c):
                dve.wait_ge(ut_sb, c + 1)
                v_tt(xT_lo[:, :], p_b[:, :], f(xT_hi[:, :]), ALU.subtract).then_inc(ut_lo, 1)

            def h_out(c):
                dve.wait_ge(f_dn, c * F + F)
                v_tt(dx[:, :], dx[:, :], p_t[:, :], ALU.add).then_inc(ho_sb, 1)

            def proj(c):
                dve.wait_ge(p_mm, c + 1)
                ch.link(c, v_tt(tok[:, 0, :, :], p_b[:, :].rearrange("p (t e) -> p t e", e=E), spread(3), ALU.add))
                stats(c, ch, lambda t: tok[:, 0, t, :], st_a, mv_a, ve_a, var_a)

            def attention(c):
                dve.wait_ge(rstd_a, c * 3 + 3)
                normalise(lambda t: tok[:, 0, t, :], lambda t: tok[:, 0, t, :], mv_a, rs_a).then_inc(att, 1)
                dve.wait_ge(att, c + 1)
                wait(dve, x1_kept, c)
                v_tt(x1[:, :, :], x_tok[:, :, :], tok[:, 0, :, :], ALU.add).then_inc(x1_sb, 1)
                dve.wait_ge(x1_sb, c + 1)
                stats(c, ch, lambda t: x1[:, t, :], st_b, mv_b, ve_b, var_x)

            def x1_norm(c):
                dve.wait_ge(rstd_x, c + 1)
                normalise(lambda t: tokb[:, t, :], lambda t: x1[:, t, :], mv_b, rs_b).then_inc(x2_tok, 1)

            def x1_turn(c):
                dve.wait_ge(x2_h, c + 1)
                v_tt(x2_lo[:, :], p_a[:, :], f(x2_hi[:, :]), ALU.subtract).then_inc(x2_l, 1)

            def route(c):
                dve.wait_ge(lg_mm, c + 1)
                ch.link(c, nc.vector.tensor_copy(lg[:, :, :], p_c[:, :].rearrange("p (t n) -> p t n", n=P)[:, :, 0:X]))
                nc.vector.nop(nofuse=True)
                for t in range(T):
                    ins = nc.vector.max(out=top[:, t, :], in_=lg[:, t, :])
                ch.link(c, ins)
                v_tt(gap[:, :], top[:, :, 0], top[:, :, 1], ALU.subtract).then_inc(gap_sb, 1)
                for t in range(T):
                    ins = nc.vector.max_index(out=idx[:, t, :], in_max=top[:, t, :], in_values=lg[:, t, :])
                ch.link(c, ins)
                nc.vector.tensor_copy(idf[:, :, :], idx[:, :, :])

            def gates_of_tokens(c):
                dve.wait_ge(th_sb, c + 1)
                v_ts(gv[:, 0, :], th[:, :], 0.5, 0.5, ALU.mult, ALU.add)
                ch.link(c, v_ts(gv[:, 1, :], th[:, :], -0.5, 0.5, ALU.mult, ALU.add))
                for t in range(T):
                    v_ts(g1[:, t, :], con[:, C_IO:C_IO + X], idf[:, t, 0:1], gv[:, 0, t:t + 1], ALU.is_equal, ALU.mult)
                    ins = v_ts(g2[:, t, :], con[:, C_IO:C_IO + X], idf[:, t, 1:2], gv[:, 1, t:t + 1],
                               ALU.is_equal, ALU.mult)
                ch.link(c, ins)
                ch.link(c, v_tt(g1[:, :, :], g1[:, :, :], g2[:, :, :], ALU.add))
                ch.link(c, nc.vector.tensor_copy(gate[:, :, 0:X].bitcast(f32r), g1[:, :, :]))
                v_tt(gate[:, :, X:2 * X], g1[:, :, :], gate[:, :, 0:X], ALU.subtract).then_inc(gate_sb, 1)

            STEPS = {"x_stats": x_stats, "x_norm": x_norm, "x_turn": x_turn, "gates": gates, "out": head_out,
                     "turn": turn, "h_var": h_var, "h_pack": h_pack, "scale": scale, "z": z, "u": u,
                     "u_turn": u_turn, "h_out": h_out, "proj": proj, "attention": attention, "x1_norm": x1_norm,
                     "x1_turn": x1_turn, "route": route, "gate": gates_of_tokens}

            def b_lo(c, i):
                dve.wait_ge(h_hi, c * NSP + splits(i))
                v_tt(g_lo[:, i % R, :], g_t[:, i % R, :], f(g_hi[:, i % R, :]), ALU.subtract).then_inc(h_lo, 1)

            def b_gated(c, e):
                dve.wait_ge(y_sb, c * NE + e + 1)
                dve.wait_ge(gb_mm, c * X + e)
                v_tt(y_e[:, :], y_e[:, :], p_g[:, :], ALU.mult).then_inc(gated, 1)

            def b_sum(c, e):
                dve.wait_ge(gated, c * X + e)
                if e >= 2:
                    dve.wait_ge(y_sum, c * X + e - 1)
                v_tt(y_acc[:, :], y_acc[:, :], y_e[:, :], ALU.add).then_inc(y_sum, 1)

            def b_out(c):
                dve.wait_ge(yt_mm, c + 1)
                stats(c, cho, lambda t: p_g[:, tile(t)], st_b, mv_b, ve_b, var_o)
                dve.wait_ge(rstd_o, c + 1)
                dve.wait_ge(res_free, c + 1)
                cho.link(c, normalise(lambda t: res[:, t, :], lambda t: p_g[:, tile(t)], mv_b, rs_b))
                dve.wait_ge(x1_kept, c + 1)
                v_tt(res[:, :, :], res[:, :, :], x1_out[:, :, :], ALU.add).then_inc(out_sb, 1)

            def body(c, ca):
                for i in range(SLOTS + 1):
                    if c is not None and i < NH and is_split(i % F):
                        b_lo(c, i)
                    if c is not None and i // F >= 2 and i % F == 2:
                        b_gated(c, i // F - 1)
                    if c is not None and i // F >= 2 and i % F == 3:
                        b_sum(c, i // F - 1)
                    if ca is not None:
                        for name, *arg in ORDER[i]:
                            if name in STEPS:
                                STEPS[name](ca, *arg)
                    if c is None and NGA + i < NG:
                        split_weights(NGA + i)
                if c is not None:
                    b_sum(c, X)
                    b_out(c)
                    cho.end()
                if ca is not None:
                    ch.end()

            for g in range(NGA):
                split_weights(g)
            selectors()
            chunks(dve, lambda: body(None, 0), body, lambda c: body(c, None))


def kernel(**inputs):
    import numpy as np
    import concourse.bacc as bacc
    from concourse.bass_utils import run_bass_kernel_spmd

    def a(name):
        return np.asarray(inputs["L0_" + name])

    mats = {"wout": lambda n, j: a("attn_Wout_w").T,
            "proj": lambda n, j: a("attn_proj_w").T,
            "d": lambda h, j: a("attn_D_w").T,
            "a": lambda h, j: a("attn_Wa_w")[h].T,
            "b": lambda h, j: a("attn_Wb_w")[h].T,
            "c": lambda h, j: a("attn_C_w")[h].T,
            "f1": lambda n, j: a("attn_ffn1_w")[n * P:(n + 1) * P].T,
            "f2": lambda n, j: a("attn_ffn2_w")[:, n * P:(n + 1) * P].T,
            "up": lambda e, j: (a("ffn_Wfc_s") if e == 0 else a("ffn_Wfc")[e - 1])[:, j * P:(j + 1) * P],
            "dn": lambda e, j: (a("ffn_Wproj_s") if e == 0 else a("ffn_Wproj")[e - 1])[j * P:(j + 1) * P]}
    weights = np.concatenate([mats[n](i, j) for n, i, j in BLOCKS], axis=1)
    native = np.concatenate([mats[n](i, j) for n, i, j in NATIVE] + [a("ffn_Wr")], axis=1)
    params = np.concatenate([
        a("attn_Wa_b").T, a("attn_Wb_b").T, a("attn_C_b").T, a("attn_D_b")[:, None], a("attn_hn_b").T,
        a("attn_ffn1_b").reshape(F, P).T, a("attn_ffn2_b")[:, None],
        a("ffn_bfc_s").reshape(F, P).T, a("ffn_bfc").reshape(X * F, P).T,
        a("ffn_bproj_s")[:, None], a("ffn_bproj").T], axis=1)
    rows = np.stack([a("attn_Wout_b"), a("attn_norm_g"), a("attn_norm_b"), a("attn_proj_b")])
    heads = np.tile(np.concatenate([a("attn_hn_g"), a("attn_head_w")[:, None]], axis=1), (SR // H, 1))

    consts = np.zeros((P, NCON), np.float32)
    consts[:, C_ID:C_ID + P] = np.eye(P)
    for h in range(H):
        consts[[h, H + h, 2 * H + h], C_HM + h] = 1
    for e in range(X):
        consts[[e, X + e], C_EM + e] = 1
    consts[0:2 * H, C_HI] = consts[3 * H:5 * H, C_HI] = 1
    consts[2 * H:3 * H, C_LO] = consts[5 * H:6 * H, C_LO] = 1
    consts[3 * H:6 * H, C_Q] = 1
    consts[:, C_IO:C_IO + X] = np.arange(X)

    arrays = {"emb": a("attn_emb").reshape(B * L, E), "weights": weights, "native": native, "params": params,
              "rows": rows, "heads": heads, "head_w": a("attn_head_w"), "consts": consts}
    arrays = {k: np.ascontiguousarray(v) for k, v in arrays.items()}
    nc = bacc.Bacc("TRN2", target_bir_lowering=False, num_devices=1)
    args = [nc.dram_tensor(k, v.shape, mybir.dt.from_np(v.dtype), kind="ExternalInput").ap()
            for k, v in arrays.items()]
    out = nc.dram_tensor("out", (B * L, E), mybir.dt.float32, kind="ExternalOutput").ap()
    build(nc, *args, out)
    r = run_bass_kernel_spmd(nc, [arrays], core_ids=[0])
    return r.results[0]["out"].reshape(B, L, E)
```

```python
from contextlib import ExitStack

import concourse.bass as bass
from concourse import mybir

P = 128
B, L, E = 4, 512, 128
T = L // P
H = 8
X = 8
F = 4
NE = X + 1
NH = NE * F
EPS = 1e-5

WA_B, WB_B, C_B, D_B, HN_B = 0, H, 2 * H, 3 * H, 3 * H + 1
F1_B = HN_B + H
F2_B = F1_B + F
FC_B = F2_B + 1
PR_B = FC_B + NH
NPAR = PR_B + NE

SR = 6 * H
C_ID, C_HM = 0, P
C_EM = C_HM + H
C_HI = C_EM + X
C_LO = C_HI + 1
C_Q = C_LO + 1
C_IO = C_Q + 1
NCON = C_IO + X

NATIVE_DOWN = 1


def is_split(j):
    return j < F - NATIVE_DOWN


def splits(i):
    return sum(is_split(k % F) for k in range(i + 1))


NSP = splits(NH - 1)

BLOCKS = [("d", 0, 0)] + [(n, h, 0) for h in range(H) for n in "ab"] + [("f1", j, 0) for j in range(F)]
NA = len(BLOCKS)
BLOCKS += [(n, e, j) for e in range(NE) for n in ("up", "dn") for j in range(F) if n == "up" or is_split(j)]
BLOCK_AT = {b: i for i, b in enumerate(BLOCKS)}
NATIVE = [("c", h, 0) for h in range(H)] + [("wout", 0, 0)] + [("f2", j, 0) for j in range(F)] + [("proj", 0, 0)]
NNA = len(NATIVE)
NATIVE += [("dn", e, j) for e in range(NE) for j in range(F) if not is_split(j)]
NATIVE_AT = {b: i for i, b in enumerate(NATIVE)}
GW = 4
GROUPS = [(s, min(s + GW, end)) for start, end in ((0, NA), (NA, len(BLOCKS))) for s in range(start, end, GW)]
NG = len(GROUPS)
NGA = -(-NA // GW)
RAW = 3
R = 3

HH = 2
HN = H // HH
LINKS_A, LINKS_G, LINKS_O = 25, 4, 3

SLOTS = NH + 2
ORDER = {i: [] for i in range(SLOTS + 1)}
PLACES = [(0, "x_stats"), (1, "x_norm"), (2, "x_turn"), (3, "dx")]
for _h in range(H + 2):
    if _h < H:
        PLACES += [(3 + _h, "gates", _h)]
    if 1 <= _h <= H:
        PLACES += [(3 + _h, "out", _h - 1)]
    if _h >= 2:
        PLACES += [(3 + _h, "turn", _h - 2)]
PLACES += [(8, "h_var", 0), (10, "h_pack", 0), (12, "h_var", 1), (15, "h_pack", 1), (16, "h_turn")]
PLACES += [(17 + _h, "scale", _h) for _h in range(H)]
PLACES += [(25, "z"), (27, "u"), (28, "u_turn"), (29, "ffn_up"), (30, "ffn_down"), (30, "h_out"),
           (31, "proj"), (33, "attention"), (35, "x1_norm"), (35, "x1_turn"), (36, "route")]
PREV = {1: "last_y", 2: "last_gated", 3: "last_sum", 4: "y_turn", 5: "out_stats", 7: "out_norm"}
OWN = {1: "gate", 3: "gate_turn"}
for _slot, *_step in PLACES:
    ORDER[_slot].append(_step)


def build(nc, emb, weights, native, params, rows, heads, head_w, consts, out):
    fp32, f32r, u32 = mybir.dt.float32, mybir.dt.float32r, mybir.dt.uint32
    ALU, ACT = mybir.AluOpType, mybir.ActivationFunctionType
    AX = mybir.AxisListType.X
    ctx = ExitStack()
    with ctx:
        def sb(name, shape, dt=fp32):
            return ctx.enter_context(nc.sbuf_tensor(name, shape, dt))

        def sem(name):
            return ctx.enter_context(nc.semaphore(name))

        w_raw = sb("w_raw", [P, RAW, GW * P])
        w_hi = sb("w_hi", [P, len(BLOCKS), P], f32r)
        w_lo = sb("w_lo", [P, len(BLOCKS), P], f32r)
        w_nat = sb("w_nat", [P, len(NATIVE), P])
        w_router = sb("w_router", [P, P])
        par = sb("par", [P, NPAR])
        row = sb("row", [P, 4, P])
        con = sb("con", [P, NCON])
        hrow = sb("hrow", [P, P + 1])
        hhi = sb("hhi", [P, P], f32r)
        hlo = sb("hlo", [P, P])
        hstack = sb("hstack", [P, P])
        hsel = sb("hsel", [P, H + 1, P], f32r)
        esel = sb("esel", [P, X, P], f32r)
        hw = sb("hw", [P, H])
        hb = sb("hb", [P, H])
        dx8_b = sb("dx8_b", [P, 1])
        mhalf = sb("mhalf", [P, T * H])

        x_tok = sb("x_tok", [P, T, E])
        tok = sb("tok", [P, 2, T, E])
        xT_hi = sb("xT_hi", [P, L], f32r)
        xT_lo = sb("xT_lo", [P, L], f32r)
        dx = sb("dx", [P, L])
        acc = sb("acc", [P, L])
        a_t = sb("a_t", [P, 2, L])
        b_t = sb("b_t", [P, L])
        o_t = sb("o_t", [P, H, L])
        st_a = sb("st_a", [P, T, 6])
        mv_a = sb("mv_a", [P, T, 2])
        ve_a = sb("ve_a", [P, T])
        rs_a = sb("rs_a", [P, T])
        st_h = sb("st_h", [P, T * H, 6])
        sm_h = sb("sm_h", [P, T * H])
        df_h = sb("df_h", [P, T * H])
        m2_h = sb("m2_h", [P, T * H])
        ve_h = sb("ve_h", [P, T * H])
        rs_h = sb("rs_h", [P, T * H])
        q_h = sb("q_h", [P, T * H])
        rq = sb("rq", [P, T, P])

        x1 = sb("x1", [P, T, E])
        x1_out = sb("x1_out", [P, T, E])
        tokb = sb("tokb", [P, T, E])
        res = sb("res", [P, T, E])
        x2_f = sb("x2_f", [P, L])
        x2_hi = sb("x2_hi", [P, L], f32r)
        x2_lo = sb("x2_lo", [P, L], f32r)
        y_acc = sb("y_acc", [P, L])
        y_e = sb("y_e", [P, L])
        g_t = sb("g_t", [P, R, L])
        g_hi = sb("g_hi", [P, R, L], f32r)
        g_lo = sb("g_lo", [P, R, L], f32r)
        st_b = sb("st_b", [P, T, 6])
        mv_b = sb("mv_b", [P, T, 2])
        ve_b = sb("ve_b", [P, T])
        rs_b = sb("rs_b", [P, T])
        lg = sb("lg", [P, T, X])
        top = sb("top", [P, T, 8])
        idx = sb("idx", [P, T, 8], u32)
        idf = sb("idf", [P, T, 8])
        gap = sb("gap", [P, T])
        th = sb("th", [P, T])
        gv = sb("gv", [P, 2, T])
        g1 = sb("g1", [P, T, X])
        g2 = sb("g2", [P, T, X])
        gate = sb("gate", [P, T, P])
        gT = sb("gT", [P, L], f32r)

        ps = [ctx.enter_context(nc.psum_tensor(f"ps{i}", [P, L], fp32)) for i in range(8)]
        p_hid, p_y, p_g = ps[0:2], ps[2], ps[3]
        p_a, p_b, p_c, p_t = ps[4:8]
        p_ffn = (p_a, p_c, p_t, p_b)

        s_raw = [sem(f"s_raw{i}") for i in range(RAW)]
        s_con, s_row, s_nat, s_natb, s_zero, s_whi, s_wlo, s_chain, s_bias, s_setup = (
            sem(n) for n in ("s_con", "s_row", "s_nat", "s_natb", "s_zero", "s_whi", "s_wlo", "s_chain", "s_bias", "s_setup"))
        x_in = sem("x_in")
        va = sem("va")
        var_a = sem("var_a")
        rstd_a = sem("rstd_a")
        var_h = sem("var_h")
        rstd_h = sem("rstd_h")
        xh = sem("xh")
        xt_mm = sem("xt_mm")
        xt_hi = sem("xt_hi")
        xt_lo = sem("xt_lo")
        dx_mm = sem("dx_mm")
        dx_sb = sem("dx_sb")
        a_mm = sem("a_mm")
        a_sb = sem("a_sb")
        b_mm = sem("b_mm")
        b_sb = sem("b_sb")
        scan = sem("scan")
        c_mm = sem("c_mm")
        o_sb = sem("o_sb")
        ot_mm = sem("ot_mm")
        o_bn = sem("o_bn")
        rq_sb = sem("rq_sb")
        rq_mm = sem("rq_mm")
        rt_sb = sem("rt_sb")
        rb_mm = sem("rb_mm")
        q_mm = sem("q_mm")
        scaled = sem("scaled")
        summed = sem("summed")
        z_mm = sem("z_mm")
        u_sb = sem("u_sb")
        ut_mm = sem("ut_mm")
        ut_sb = sem("ut_sb")
        ut_lo = sem("ut_lo")
        f_mm = sem("f_mm")
        f_sb = sem("f_sb")
        f_dn = sem("f_dn")
        ho_sb = sem("ho_sb")
        p_mm = sem("p_mm")
        att = sem("att")
        x1_sb = sem("x1_sb")
        x1_kept = sem("x1_kept")
        var_x = sem("var_x")
        rstd_x = sem("rstd_x")
        x2_tok = sem("x2_tok")
        x2_mm = sem("x2_mm")
        x2_h = sem("x2_h")
        x2_l = sem("x2_l")
        lg_mm = sem("lg_mm")
        gap_sb = sem("gap_sb")
        th_sb = sem("th_sb")
        gate_sb = sem("gate_sb")
        gt_mm = sem("gt_mm")
        gt_sb = sem("gt_sb")
        vg = sem("vg")
        up_mm = sem("up_mm")
        h_sb = sem("h_sb")
        h_hi = sem("h_hi")
        h_lo = sem("h_lo")
        dn_mm = sem("dn_mm")
        y_sb = sem("y_sb")
        gb_mm = sem("gb_mm")
        gated = sem("gated")
        y_sum = sem("y_sum")
        yt_mm = sem("yt_mm")
        vo = sem("vo")
        var_o = sem("var_o")
        rstd_o = sem("rstd_o")
        out_sb = sem("out_sb")
        stored = sem("stored")
        res_free = sem("res_free")

        def ident():
            return con[:, C_ID:C_ID + P]

        def col(k):
            return par[:, k:k + 1]

        def tile(t):
            return slice(t * P, (t + 1) * P)

        def wait(eng, s, value):
            if not isinstance(value, int) or value > 0:
                eng.wait_ge(s, value)

        def chunks(eng, body, rest):
            body(None, 0)
            body(0, 1)
            with eng.Fori(1, B - 1) as c:
                body(c, c + 1)
            body(B - 1, None)
            rest(B - 1)

        def is_first(c):
            return isinstance(c, int) and c == 0

        block = ctx.enter_context(nc.Block())

        @block.sync
        def _(sp):
            def load(c):
                wait(sp, x1_sb, c)
                sp.dma_start(x_tok[:, :, :],
                             emb[bass.ds(c * L, L), :].rearrange("(t p) e -> p t e", p=P)).then_inc(x_in, 16)

            def store(c):
                sp.wait_ge(out_sb, c + 1)
                sp.dma_start(out[bass.ds(c * L, L), :].rearrange("(t p) e -> p t e", p=P),
                             res[:, :, :]).then_inc(stored, 16)
                sp.wait_ge(stored, c * 16 + 16)
                sp.sem_inc(res_free, 1)

            load(0)
            sp.dma_start(con[:, :], consts).then_inc(s_con, 16)
            sp.dma_start(par[:, :], params).then_inc(s_con, 16)
            sp.dma_start(hw[:, :], head_w.partition_broadcast(P)).then_inc(s_con, 16)
            sp.sem_inc(res_free, 1)
            for g, (b0, b1) in enumerate(GROUPS):
                if g >= RAW:
                    sp.wait_ge(s_wlo, g - RAW + 1)
                sp.dma_start(w_raw[:, g % RAW, 0:(b1 - b0) * P],
                             weights[:, b0 * P:b1 * P]).then_inc(s_raw[g % RAW], 16)
                if g == RAW - 1:
                    sp.dma_start(hrow[0:SR, :], heads).then_inc(s_row, 16)
                    sp.dma_start(w_nat[:, 0:NNA, :],
                                 native[:, 0:NNA * P].rearrange("p (n e) -> p n e", e=P)).then_inc(s_nat, 16)
                    sp.dma_start(row[:, :, :], rows.partition_broadcast(P)).then_inc(s_row, 16)
                if g == NGA:
                    sp.wait_ge(s_zero, 3)
                    sp.dma_start(w_router[:, 0:X],
                                 native[:, len(NATIVE) * P:len(NATIVE) * P + X]).then_inc(s_natb, 16)
                    sp.dma_start(w_nat[:, NNA:, :],
                                 native[:, NNA * P:len(NATIVE) * P].rearrange("p (n e) -> p n e", e=P)
                                 ).then_inc(s_natb, 16)
            load(1)
            with sp.Fori(1, B - 1) as c:
                load(c + 1)
                store(c - 1)
            store(B - 2)
            store(B - 1)
            sp.wait_ge(stored, B * 16)

        @block.gpsimd
        def _(pool):
            nc.gpsimd.memset(mhalf[:, :], -0.5).then_inc(s_zero, 1)
            nc.gpsimd.memset(hstack[:, :], 0.0).then_inc(s_zero, 1)
            nc.gpsimd.memset(w_router[:, :], 0.0).then_inc(s_zero, 1)
            nc.gpsimd.memset(rq[:, :, :], 0.0).then_inc(s_zero, 1)
            nc.gpsimd.memset(gate[:, :, :], 0.0).then_inc(s_zero, 1)
            pool.wait_ge(s_zero, 5)

            def rstd(out_, var, var_ready, n, done):
                pool.wait_ge(var_ready, n)
                nc.gpsimd.tensor_tensor(out=out_, in0=var, in1=mhalf[:, 0:out_.shape[1]],
                                        op=ALU.pow).then_inc(done, 1)

            def x_norm(c):
                rstd(rs_a[:, :], ve_a[:, :], var_a, c * 3 + 1, rstd_a)

            def a_norms(c):
                for k in range(HH):
                    half = slice(k * T * HN, (k + 1) * T * HN)
                    rstd(rs_h[:, half], ve_h[:, half], var_h, c * HH + k + 1, rstd_h)
                rstd(rs_a[:, :], ve_a[:, :], var_a, c * 3 + 2, rstd_a)
                rstd(rs_a[:, :], ve_a[:, :], var_a, c * 3 + 3, rstd_a)
                rstd(rs_b[:, :], ve_b[:, :], var_x, c + 1, rstd_x)

            def keep(c):
                pool.wait_ge(x1_sb, c + 1)
                wait(pool, out_sb, c)
                nc.gpsimd.nop(nofuse=True)
                nc.gpsimd.tensor_copy(x1_out[:, :, :], x1[:, :, :]).then_inc(x1_kept, 1)

            def out_norm(c):
                rstd(rs_b[:, :], ve_b[:, :], var_o, c + 1, rstd_o)

            def body(c, ca):
                if ca is not None:
                    x_norm(ca)
                if c is not None:
                    if not is_first(c):
                        out_norm(c - 1)
                    keep(c)
                if ca is not None:
                    a_norms(ca)

            chunks(pool, body, out_norm)

        @block.tensor
        def _(pe):
            def mm3(dst, name, x_hi, x_lo, start=True, stop=True):
                w = BLOCK_AT[name]
                nc.tensor.matmul(dst, w_hi[:, w, :], x_hi, start=start, stop=False)
                nc.tensor.matmul(dst, w_lo[:, w, :], x_hi, start=False, stop=False)
                return nc.tensor.matmul(dst, w_hi[:, w, :], x_lo, start=False, stop=stop)

            def transposes(dst, src):
                for t in range(T):
                    last = nc.tensor.transpose(dst[:, tile(t)], src(t), ident())
                return last

            def x_turn(c):
                pe.wait_ge(xh, c + 1)
                transposes(p_a, lambda t: tok[:, 0, t, :]).then_inc(xt_mm, 1)

            def dx_product(c):
                pe.wait_ge(xt_lo, c + 1)
                wait(pe, gap_sb, c)
                if is_first(c):
                    pe.wait_ge(s_wlo, 1)
                mm3(p_c[:, :], ("d", 0, 0), xT_hi[:, :], xT_lo[:, :]).then_inc(dx_mm, 1)

            def gates(c, h):
                if h > 0:
                    pe.wait_ge(a_sb, c * H + h)
                if is_first(c):
                    pe.wait_ge(s_wlo, BLOCK_AT["b", h, 0] // GW + 1)
                mm3(p_a[:, :], ("a", h, 0), xT_hi[:, :], xT_lo[:, :]).then_inc(a_mm, 1)
                if h > 0:
                    pe.wait_ge(b_sb, c * H + h)
                mm3(p_b[:, :], ("b", h, 0), xT_hi[:, :], xT_lo[:, :]).then_inc(b_mm, 1)

            def head_out(c, h):
                pe.wait_ge(scan, c * H + h + 1)
                if h == 0:
                    pe.wait_ge(dx_sb, c + 1)
                    if is_first(c):
                        pe.wait_ge(s_nat, 16)
                else:
                    pe.wait_ge(o_sb, c * H + h)
                nc.tensor.matmul(p_c[:, :], w_nat[:, NATIVE_AT["c", h, 0], :], o_t[:, h, :],
                                 start=True, stop=True).then_inc(c_mm, 1)

            def turn(c, h):
                pe.wait_ge(o_sb, c * H + h + 1)
                if h > 0:
                    pe.wait_ge(o_bn, c * H + h)
                else:
                    wait(pe, gt_sb, c)
                transposes(p_t, lambda t: o_t[:, h, tile(t)]).then_inc(ot_mm, 1)

            def h_turn(c):
                pe.wait_ge(rq_sb, c * HH + HH)
                transposes(p_t, lambda t: rq[:, t, :]).then_inc(rq_mm, 1)

            def scale(c, h):
                if h == 0:
                    pe.wait_ge(rt_sb, c + 1)
                    if is_first(c):
                        pe.wait_ge(s_setup, 1)
                if h >= 2:
                    pe.wait_ge(scaled, c * H + h - 1)
                nc.tensor.matmul((p_a, p_b)[h % 2][:, :], hsel[:, h, :], xT_hi[:, :],
                                 start=True, stop=True).then_inc(rb_mm, 1)
                if h == 1:
                    nc.tensor.matmul(p_c[:, :], hsel[:, H, :], xT_hi[:, :], start=True, stop=True).then_inc(q_mm, 1)

            def z(c):
                pe.wait_ge(summed, c * (H + 1) + H + 1)
                for t in range(T):
                    last = nc.tensor.matmul(p_a[:, tile(t)], acc[:, tile(t)], w_nat[:, NATIVE_AT["wout", 0, 0], :],
                                            start=True, stop=True)
                last.then_inc(z_mm, 1)

            def u_turn(c):
                pe.wait_ge(u_sb, c + 1)
                transposes(p_b, lambda t: tok[:, 1, t, :]).then_inc(ut_mm, 1)

            def ffn_up(c):
                pe.wait_ge(ut_lo, c + 1)
                if is_first(c):
                    pe.wait_ge(s_wlo, NGA)
                for j in range(F):
                    mm3(p_ffn[j][:, :], ("f1", j, 0), xT_hi[:, :], xT_lo[:, :]).then_inc(f_mm, 1)

            def ffn_down(c):
                for j in range(F):
                    pe.wait_ge(f_sb, c * F + j + 1)
                    ins = nc.tensor.matmul(p_a[:, :], w_nat[:, NATIVE_AT["f2", j, 0], :], o_t[:, j, :],
                                           start=(j == 0), stop=(j == F - 1))
                ins.then_inc(f_dn, 1)

            def proj(c):
                pe.wait_ge(ho_sb, c + 1)
                for t in range(T):
                    last = nc.tensor.matmul(p_b[:, tile(t)], dx[:, tile(t)], w_nat[:, NATIVE_AT["proj", 0, 0], :],
                                            start=True, stop=True)
                last.then_inc(p_mm, 1)

            def x1_turn(c):
                pe.wait_ge(x2_tok, c + 1)
                transposes(p_a, lambda t: tokb[:, t, :]).then_inc(x2_mm, 1)

            def route(c):
                pe.wait_ge(x2_h, c + 1)
                if is_first(c):
                    pe.wait_ge(s_natb, 32)
                for t in range(T):
                    last = nc.tensor.matmul(p_c[:, tile(t)], x2_f[:, tile(t)], w_router[:, :], start=True, stop=True)
                last.then_inc(lg_mm, 1)

            def gate_turn(c):
                pe.wait_ge(gate_sb, c + 1)
                transposes(p_t, lambda t: gate[:, t, :]).then_inc(gt_mm, 1)

            STEPS = {"x_turn": x_turn, "dx": dx_product, "gates": gates, "out": head_out, "turn": turn,
                     "h_turn": h_turn, "scale": scale, "z": z, "u_turn": u_turn, "ffn_up": ffn_up,
                     "ffn_down": ffn_down, "proj": proj, "x1_turn": x1_turn, "route": route, "gate_turn": gate_turn}

            def b_up(c, i):
                if i == 0:
                    pe.wait_ge(x2_l, c + 1)
                    if is_first(c):
                        pe.wait_ge(s_wlo, NG)
                if i >= 2 or not is_first(c):
                    pe.wait_ge(h_sb, c * NH + i - 1)
                mm3(p_hid[i % 2][:, :], ("up", i // F, i % F), x2_hi[:, :], x2_lo[:, :]).then_inc(up_mm, 1)

            def b_gate_bc(c, e):
                if e == 1:
                    pe.wait_ge(gt_sb, c + 1)
                    wait(pe, out_sb, c)
                else:
                    pe.wait_ge(gated, c * X + e - 1)
                nc.tensor.matmul(p_g[:, :], esel[:, e - 1, :], gT[:, :], start=True, stop=True).then_inc(gb_mm, 1)

            def b_down(c, i):
                e, j = i // F, i % F
                if j == 0:
                    wait(pe, y_sb, c * NE + e)
                first, last = j == 0, j == F - 1
                if is_split(j):
                    pe.wait_ge(h_lo, c * NSP + splits(i))
                    ins = mm3(p_y[:, :], ("dn", e, j), g_hi[:, i % R, :], g_lo[:, i % R, :], start=first, stop=last)
                else:
                    pe.wait_ge(h_sb, c * NH + i + 1)
                    ins = nc.tensor.matmul(p_y[:, :], w_nat[:, NATIVE_AT["dn", e, j], :], g_t[:, i % R, :],
                                           start=first, stop=last)
                ins.then_inc(dn_mm, 1)

            def y_turn(c):
                pe.wait_ge(y_sum, c * X + X)
                transposes(p_g, lambda t: y_acc[:, tile(t)]).then_inc(yt_mm, 1)

            LEFT = {"y_turn": y_turn}

            def body(c, ca):
                for i in range(SLOTS):
                    if c is not None and i < NH:
                        b_up(c, i)
                    if c is not None and i >= 2:
                        b_down(c, i - 2)
                        if (i - 2) % F == 2 and i - 2 >= F:
                            b_gate_bc(c, (i - 2) // F)
                    if c is not None and not is_first(c) and PREV.get(i) in LEFT:
                        LEFT[PREV[i]](c - 1)
                    if c is not None and OWN.get(i) in STEPS:
                        STEPS[OWN[i]](c)
                    if ca is not None:
                        for name, *arg in ORDER[i]:
                            if name in STEPS:
                                STEPS[name](ca, *arg)

            pe.wait_ge(s_con, 3 * 16)
            pe.wait_ge(s_zero, 5)
            chunks(pe, body, y_turn)

        @block.scalar
        def _(act):
            def copy(dst, src):
                return nc.scalar.activation(dst, src, ACT.Copy)

            def split_weights(g):
                b0, b1 = GROUPS[g]
                act.wait_ge(s_raw[g % RAW], 16 * (g // RAW + 1))
                copy(w_hi[:, b0:b1, :], w_raw[:, g % RAW, 0:(b1 - b0) * P]
                     .rearrange("p (b n) -> p b n", n=P)).then_inc(s_whi, 1)

            def x_turn(c):
                act.wait_ge(xt_mm, c + 1)
                copy(xT_hi[:, :], p_a[:, :]).then_inc(xt_hi, 1)

            def dx_start(c):
                act.wait_ge(dx_mm, c + 1)
                nc.scalar.activation(dx[:, :], p_c[:, :], ACT.Identity, bias=col(D_B))
                if is_first(c):
                    act.wait_ge(s_bias, 1)
                nc.scalar.activation(acc[:, :], p_c[:, :], ACT.Identity, bias=dx8_b[:, :],
                                     scale=1.0 / H).then_inc(dx_sb, 1)

            def gates(c, h):
                act.wait_ge(a_mm, c * H + h + 1)
                if h >= 2:
                    act.wait_ge(scan, c * H + h - 1)
                nc.scalar.activation(a_t[:, h % 2, :], p_a[:, :], ACT.Tanh, bias=col(WA_B + h)).then_inc(a_sb, 1)
                act.wait_ge(b_mm, c * H + h + 1)
                if h >= 1:
                    act.wait_ge(scan, c * H + h)
                nc.scalar.activation(b_t[:, :], p_b[:, :], ACT.Identity, bias=col(WB_B + h)).then_inc(b_sb, 1)

            def h_turn(c):
                act.wait_ge(rq_mm, c + 1)
                copy(xT_hi[:, :], p_t[:, :]).then_inc(rt_sb, 1)

            def u_turn(c):
                act.wait_ge(ut_mm, c + 1)
                copy(xT_hi[:, :], p_b[:, :])
                nc.scalar.activation(dx[:, :], p_b[:, :], ACT.Identity, bias=col(F2_B)).then_inc(ut_sb, 1)

            def ffn_up(c):
                for j in range(F):
                    act.wait_ge(f_mm, c * F + j + 1)
                    nc.scalar.activation(o_t[:, j, :], p_ffn[j][:, :], ACT.Gelu, bias=col(F1_B + j)).then_inc(f_sb, 1)

            def x1_turn(c):
                act.wait_ge(x2_mm, c + 1)
                wait(act, up_mm, c * NH)
                copy(x2_hi[:, :], p_a[:, :])
                copy(x2_f[:, :], p_a[:, :]).then_inc(x2_h, 1)

            def gate(c):
                act.wait_ge(gap_sb, c + 1)
                nc.scalar.activation(th[:, :], gap[:, :], ACT.Tanh, scale=0.5).then_inc(th_sb, 1)

            def gate_turn(c):
                act.wait_ge(gt_mm, c + 1)
                copy(gT[:, :], p_t[:, :]).then_inc(gt_sb, 1)

            STEPS = {"x_turn": x_turn, "dx": dx_start, "gates": gates, "h_turn": h_turn, "u_turn": u_turn,
                     "ffn_up": ffn_up, "x1_turn": x1_turn, "gate": gate, "gate_turn": gate_turn}

            def b_gelu(c, i):
                act.wait_ge(up_mm, c * NH + i + 1)
                nc.scalar.activation(g_t[:, i % R, :], p_hid[i % 2][:, :], ACT.Gelu_apprx_tanh,
                                     bias=col(FC_B + i)).then_inc(h_sb, 1)

            def b_hi(c, i):
                act.wait_ge(h_sb, c * NH + i + 1)
                copy(g_hi[:, i % R, :], g_t[:, i % R, :]).then_inc(h_hi, 1)

            def b_y(c, e):
                act.wait_ge(dn_mm, c * NH + e * F + F)
                if e == 0:
                    wait(act, yt_mm, c)
                elif e >= 2:
                    act.wait_ge(y_sum, c * X + e - 1)
                nc.scalar.activation((y_e if e else y_acc)[:, :], p_y[:, :], ACT.Identity,
                                     bias=col(PR_B + e)).then_inc(y_sb, 1)

            def last_y(c):
                b_y(c, X)

            LEFT = {"last_y": last_y}

            def body(c, ca):
                for i in range(SLOTS):
                    if c is not None and i < NH:
                        b_gelu(c, i)
                        if is_split(i % F):
                            b_hi(c, i)
                    if c is not None and i % F == 1 and F < i < NH:
                        b_y(c, i // F - 1)
                    if c is not None and not is_first(c) and PREV.get(i) in LEFT:
                        LEFT[PREV[i]](c - 1)
                    if c is not None and OWN.get(i) in STEPS:
                        STEPS[OWN[i]](c)
                    if ca is not None:
                        for name, *arg in ORDER[i]:
                            if name in STEPS:
                                STEPS[name](ca, *arg)
                    if c is None and i < NG:
                        split_weights(i)

            act.wait_ge(s_con, 3 * 16)
            chunks(act, body, last_y)

        @block.vector
        def _(dve):
            def f(ap):
                return ap.bitcast(fp32)

            class Chain:

                def __init__(self, s, links):
                    self.s, self.links, self.k = s, links, 0

                def link(self, c, ins):
                    self.k += 1
                    ins.then_inc(self.s, 1)
                    dve.wait_ge(self.s, c * self.links + self.k)

                def end(self):
                    assert self.k == self.links, (self.k, self.links)
                    self.k = 0

            ch, chg, cho = Chain(va, LINKS_A), Chain(vg, LINKS_G), Chain(vo, LINKS_O)

            def v_tt(dst, a, b, op):
                return nc.vector.tensor_tensor(out=dst, in0=a, in1=b, op=op)

            def v_ts(dst, a, s1, s2, op0, op1):
                return nc.vector.tensor_scalar(out=dst, in0=a, scalar1=s1, scalar2=s2, op0=op0, op1=op1)

            def split_weights(g):
                b0, b1 = GROUPS[g]
                dve.wait_ge(s_whi, g + 1)
                v_tt(w_lo[:, b0:b1, :], w_raw[:, g % RAW, 0:(b1 - b0) * P].rearrange("p (b n) -> p b n", n=P),
                     f(w_hi[:, b0:b1, :]), ALU.subtract).then_inc(s_wlo, 1)

            setup = [0]

            def link(ins):
                setup[0] += 1
                ins.then_inc(s_chain, 1)
                dve.wait_ge(s_chain, setup[0])

            def head_bias():
                dve.wait_ge(s_con, 3 * 16)
                link(v_tt(hb[:, :], par[:, HN_B:HN_B + H], hw[:, :], ALU.mult))
                link(nc.vector.reduce_sum(dx8_b[:, :], hb[:, :], axis=AX))
                link(v_tt(dx8_b[:, :], dx8_b[:, :], col(D_B), ALU.add))
                v_ts(dx8_b[:, :], dx8_b[:, :], 1.0 / H, None, ALU.mult, ALU.bypass).then_inc(s_bias, 1)

            def selectors():
                dve.wait_ge(s_row, 2 * 16)
                dve.wait_ge(s_zero, 5)
                link(v_ts(hrow[0:SR, 0:P], hrow[0:SR, 0:P], hrow[0:SR, P:P + 1], 1.0 / H, ALU.mult, ALU.mult))
                link(nc.vector.tensor_copy(hhi[0:SR, :], hrow[0:SR, 0:P]))
                link(v_tt(hlo[0:SR, :], hrow[0:SR, 0:P], f(hhi[0:SR, :]), ALU.subtract))
                link(v_ts(hlo[0:SR, :], hlo[0:SR, :], con[0:SR, C_LO:C_LO + 1], None, ALU.mult, ALU.bypass))
                link(nc.vector.scalar_tensor_tensor(out=hstack[0:SR, :], in0=f(hhi[0:SR, :]),
                                                    scalar=con[0:SR, C_HI:C_HI + 1], in1=hlo[0:SR, :],
                                                    op0=ALU.mult, op1=ALU.add))
                for h in range(H):
                    v_ts(hsel[:, h, :], hstack[:, :], con[:, C_HM + h:C_HM + h + 1], None, ALU.mult, ALU.bypass)
                v_ts(hsel[:, H, :], hstack[:, :], con[:, C_Q:C_Q + 1], None, ALU.mult, ALU.bypass)
                nc.vector.tensor_copy(esel[:, :, :],
                                      con[:, C_EM:C_EM + X].unsqueeze(2).to_broadcast([P, X, P])).then_inc(s_setup, 1)

            def stats(c, chain, src, st, mv, ve, ready):
                for t in range(T):
                    ins = nc.vector.bn_stats(out=st[:, t, :], in_=src(t))
                chain.link(c, ins)
                nc.vector.nop(nofuse=True)
                for t in range(T):
                    ins = nc.vector.bn_aggr(out=mv[:, t, :], in_=st[:, t, :])
                chain.link(c, ins)
                nc.vector.tensor_scalar_add(ve[:, :], mv[:, :, 1], EPS).then_inc(ready, 1)

            def normalise(dst, src, mv, rs):
                for t in range(T):
                    ins = v_ts(dst(t), src(t), mv[:, t, 0:1], rs[:, t:t + 1], ALU.subtract, ALU.mult)
                return ins

            def spread(r):
                return row[:, r:r + 1, :].to_broadcast([P, T, P])

            def x_stats(c):
                dve.wait_ge(x_in, c * 16 + 16)
                stats(c, ch, lambda t: x_tok[:, t, :], st_a, mv_a, ve_a, var_a)

            def x_norm(c):
                dve.wait_ge(rstd_a, c * 3 + 1)
                normalise(lambda t: tok[:, 0, t, :], lambda t: x_tok[:, t, :], mv_a, rs_a).then_inc(xh, 1)

            def x_turn(c):
                dve.wait_ge(xt_hi, c + 1)
                v_tt(xT_lo[:, :], p_a[:, :], f(xT_hi[:, :]), ALU.subtract).then_inc(xt_lo, 1)

            def gates(c, h):
                dve.wait_ge(b_sb, c * H + h + 1)
                nc.vector.tensor_tensor_scan(out=o_t[:, h, :], data0=a_t[:, h % 2, :], data1=b_t[:, :],
                                             initial=0.0, op0=ALU.mult, op1=ALU.add).then_inc(scan, 1)

            def head_out(c, h):
                dve.wait_ge(c_mm, c * H + h + 1)
                nc.vector.scalar_tensor_tensor(out=o_t[:, h, :], in0=p_c[:, :], scalar=col(C_B + h), in1=dx[:, :],
                                               op0=ALU.add, op1=ALU.mult).then_inc(o_sb, 1)

            def turn(c, h):
                dve.wait_ge(ot_mm, c * H + h + 1)
                for t in range(T):
                    ins = nc.vector.bn_stats(out=st_h[:, (h // HN * T + t) * HN + h % HN, :], in_=p_t[:, tile(t)])
                ins.then_inc(o_bn, 1)

            def h_var(c, k):
                half = slice(k * T * HN, (k + 1) * T * HN)
                dve.wait_ge(o_bn, c * H + (k + 1) * HN)
                me, m2e, mo, m2o = (st_h[:, half, n] for n in (1, 2, 4, 5))
                v_tt(df_h[:, half], me, mo, ALU.subtract)
                v_tt(sm_h[:, half], me, mo, ALU.add)
                ch.link(c, v_tt(m2_h[:, half], m2e, m2o, ALU.add))
                ch.link(c, v_tt(df_h[:, half], df_h[:, half], df_h[:, half], ALU.mult))
                ch.link(c, v_ts(df_h[:, half], df_h[:, half], 0.25, EPS, ALU.mult, ALU.add))
                nc.vector.scalar_tensor_tensor(out=ve_h[:, half], in0=m2_h[:, half], scalar=1.0 / P,
                                               in1=df_h[:, half], op0=ALU.mult, op1=ALU.add).then_inc(var_h, 1)

            def h_pack(c, k):
                half = slice(k * T * HN, (k + 1) * T * HN)
                dve.wait_ge(rstd_h, c * HH + k + 1)
                r = rs_h[:, half].rearrange("p (t h) -> p t h", h=HN)
                q = q_h[:, half].rearrange("p (t h) -> p t h", h=HN)

                def part(n):
                    return rq[:, :, n * H + k * HN:n * H + (k + 1) * HN]

                nc.vector.tensor_copy(part(0).bitcast(f32r), r)
                nc.vector.tensor_copy(part(2).bitcast(f32r), r)
                ch.link(c, nc.vector.scalar_tensor_tensor(out=q_h[:, half], in0=sm_h[:, half], scalar=-0.5,
                                                          in1=rs_h[:, half], op0=ALU.mult, op1=ALU.mult))
                v_tt(part(1), r, part(0), ALU.subtract)
                nc.vector.tensor_copy(part(5).bitcast(f32r), q)
                ch.link(c, nc.vector.tensor_copy(part(3).bitcast(f32r), q))
                v_tt(part(4), q, part(3), ALU.subtract).then_inc(rq_sb, 1)

            def scale(c, h):
                dve.wait_ge(rb_mm, c * H + h + 1)
                v_tt(o_t[:, h, :], o_t[:, h, :], (p_a, p_b)[h % 2][:, :], ALU.mult).then_inc(scaled, 1)
                if h == 1:
                    dve.wait_ge(q_mm, c + 1)
                    v_tt(acc[:, :], acc[:, :], p_c[:, :], ALU.add).then_inc(summed, 1)
                if h >= 1:
                    add_head(c, h - 1)
                if h == H - 1:
                    add_head(c, h)

            def add_head(c, h):
                dve.wait_ge(scaled, c * H + h + 1)
                dve.wait_ge(summed, c * (H + 1) + h + 1)
                v_tt(acc[:, :], acc[:, :], o_t[:, h, :], ALU.add).then_inc(summed, 1)

            def z(c):
                dve.wait_ge(z_mm, c + 1)
                ch.link(c, v_tt(tok[:, 0, :, :], p_a[:, :].rearrange("p (t e) -> p t e", e=E), spread(0), ALU.add))
                stats(c, ch, lambda t: tok[:, 0, t, :], st_a, mv_a, ve_a, var_a)
                ch.link(c, v_tt(tok[:, 1, :, :], tok[:, 0, :, :], spread(2), ALU.add))
                for t in range(T):
                    ins = nc.vector.scalar_tensor_tensor(out=tok[:, 0, t, :], in0=tok[:, 0, t, :],
                                                         scalar=mv_a[:, t, 0:1], in1=row[:, 1, :],
                                                         op0=ALU.subtract, op1=ALU.mult)
                ch.link(c, ins)

            def u(c):
                dve.wait_ge(rstd_a, c * 3 + 2)
                for t in range(T):
                    ins = nc.vector.scalar_tensor_tensor(out=tok[:, 1, t, :], in0=tok[:, 0, t, :],
                                                         scalar=rs_a[:, t:t + 1], in1=tok[:, 1, t, :],
                                                         op0=ALU.mult, op1=ALU.add)
                ins.then_inc(u_sb, 1)

            def u_turn(c):
                dve.wait_ge(ut_sb, c + 1)
                v_tt(xT_lo[:, :], p_b[:, :], f(xT_hi[:, :]), ALU.subtract).then_inc(ut_lo, 1)

            def h_out(c):
                dve.wait_ge(f_dn, c + 1)
                v_tt(dx[:, :], dx[:, :], p_a[:, :], ALU.add).then_inc(ho_sb, 1)

            def proj(c):
                dve.wait_ge(p_mm, c + 1)
                ch.link(c, v_tt(tok[:, 0, :, :], p_b[:, :].rearrange("p (t e) -> p t e", e=E), spread(3), ALU.add))
                stats(c, ch, lambda t: tok[:, 0, t, :], st_a, mv_a, ve_a, var_a)

            def attention(c):
                dve.wait_ge(rstd_a, c * 3 + 3)
                normalise(lambda t: tok[:, 0, t, :], lambda t: tok[:, 0, t, :], mv_a, rs_a).then_inc(att, 1)
                dve.wait_ge(att, c + 1)
                wait(dve, x1_kept, c)
                v_tt(x1[:, :, :], x_tok[:, :, :], tok[:, 0, :, :], ALU.add).then_inc(x1_sb, 1)
                dve.wait_ge(x1_sb, c + 1)
                stats(c, ch, lambda t: x1[:, t, :], st_b, mv_b, ve_b, var_x)

            def x1_norm(c):
                dve.wait_ge(rstd_x, c + 1)
                normalise(lambda t: tokb[:, t, :], lambda t: x1[:, t, :], mv_b, rs_b).then_inc(x2_tok, 1)

            def x1_turn(c):
                dve.wait_ge(x2_h, c + 1)
                v_tt(x2_lo[:, :], p_a[:, :], f(x2_hi[:, :]), ALU.subtract).then_inc(x2_l, 1)

            def route(c):
                dve.wait_ge(lg_mm, c + 1)
                ch.link(c, nc.vector.tensor_copy(lg[:, :, :], p_c[:, :].rearrange("p (t n) -> p t n", n=P)[:, :, 0:X]))
                nc.vector.nop(nofuse=True)
                for t in range(T):
                    ins = nc.vector.max(out=top[:, t, :], in_=lg[:, t, :])
                ch.link(c, ins)
                v_tt(gap[:, :], top[:, :, 0], top[:, :, 1], ALU.subtract).then_inc(gap_sb, 1)
                for t in range(T):
                    ins = nc.vector.max_index(out=idx[:, t, :], in_max=top[:, t, :], in_values=lg[:, t, :])
                ch.link(c, ins)
                nc.vector.tensor_copy(idf[:, :, :], idx[:, :, :])

            def gates_of_tokens(c):
                dve.wait_ge(th_sb, c + 1)
                v_ts(gv[:, 0, :], th[:, :], 0.5, 0.5, ALU.mult, ALU.add)
                chg.link(c, v_ts(gv[:, 1, :], th[:, :], -0.5, 0.5, ALU.mult, ALU.add))
                for t in range(T):
                    v_ts(g1[:, t, :], con[:, C_IO:C_IO + X], idf[:, t, 0:1], gv[:, 0, t:t + 1], ALU.is_equal, ALU.mult)
                    ins = v_ts(g2[:, t, :], con[:, C_IO:C_IO + X], idf[:, t, 1:2], gv[:, 1, t:t + 1],
                               ALU.is_equal, ALU.mult)
                chg.link(c, ins)
                chg.link(c, v_tt(g1[:, :, :], g1[:, :, :], g2[:, :, :], ALU.add))
                chg.link(c, nc.vector.tensor_copy(gate[:, :, 0:X].bitcast(f32r), g1[:, :, :]))
                v_tt(gate[:, :, X:2 * X], g1[:, :, :], gate[:, :, 0:X], ALU.subtract).then_inc(gate_sb, 1)

            STEPS = {"x_stats": x_stats, "x_norm": x_norm, "x_turn": x_turn, "gates": gates, "out": head_out,
                     "turn": turn, "h_var": h_var, "h_pack": h_pack, "scale": scale, "z": z, "u": u,
                     "u_turn": u_turn, "h_out": h_out, "proj": proj, "attention": attention, "x1_norm": x1_norm,
                     "x1_turn": x1_turn, "route": route, "gate": gates_of_tokens}

            def b_lo(c, i):
                dve.wait_ge(h_hi, c * NSP + splits(i))
                v_tt(g_lo[:, i % R, :], g_t[:, i % R, :], f(g_hi[:, i % R, :]), ALU.subtract).then_inc(h_lo, 1)

            def b_gated(c, e):
                dve.wait_ge(y_sb, c * NE + e + 1)
                dve.wait_ge(gb_mm, c * X + e)
                v_tt(y_e[:, :], y_e[:, :], p_g[:, :], ALU.mult).then_inc(gated, 1)

            def b_sum(c, e):
                dve.wait_ge(gated, c * X + e)
                if e >= 2:
                    dve.wait_ge(y_sum, c * X + e - 1)
                v_tt(y_acc[:, :], y_acc[:, :], y_e[:, :], ALU.add).then_inc(y_sum, 1)

            def last_gated(c):
                b_gated(c, X)

            def last_sum(c):
                b_sum(c, X)

            def out_stats(c):
                dve.wait_ge(yt_mm, c + 1)
                stats(c, cho, lambda t: p_g[:, tile(t)], st_b, mv_b, ve_b, var_o)

            def out_norm(c):
                dve.wait_ge(rstd_o, c + 1)
                dve.wait_ge(res_free, c + 1)
                cho.link(c, normalise(lambda t: res[:, t, :], lambda t: p_g[:, tile(t)], mv_b, rs_b))
                dve.wait_ge(x1_kept, c + 1)
                v_tt(res[:, :, :], res[:, :, :], x1_out[:, :, :], ALU.add).then_inc(out_sb, 1)
                cho.end()

            LEFT = {"last_gated": last_gated, "last_sum": last_sum, "out_stats": out_stats, "out_norm": out_norm}

            def body(c, ca):
                for i in range(SLOTS):
                    if c is not None and i < NH and is_split(i % F):
                        b_lo(c, i)
                    if c is not None and i // F >= 2 and i < NH and i % F == 2:
                        b_gated(c, i // F - 1)
                    if c is not None and i // F >= 2 and i < NH and i % F == 3:
                        b_sum(c, i // F - 1)
                    if c is not None and not is_first(c) and PREV.get(i) in LEFT:
                        LEFT[PREV[i]](c - 1)
                    if c is not None and OWN.get(i) in STEPS:
                        STEPS[OWN[i]](c)
                        chg.end()
                    if ca is not None:
                        for name, *arg in ORDER[i]:
                            if name in STEPS:
                                STEPS[name](ca, *arg)
                    if c is None and i < NG:
                        split_weights(i)
                    if c is None and i == 0:
                        head_bias()
                    if c is None and i == H:
                        selectors()
                if ca is not None:
                    ch.end()

            def rest(c):
                last_gated(c)
                last_sum(c)
                out_stats(c)
                out_norm(c)

            chunks(dve, body, rest)


def kernel(**inputs):
    import numpy as np
    import concourse.bacc as bacc
    from concourse.bass_utils import run_bass_kernel_spmd

    def a(name):
        return np.asarray(inputs["L0_" + name])

    mats = {"wout": lambda n, j: a("attn_Wout_w").T,
            "proj": lambda n, j: a("attn_proj_w").T,
            "d": lambda h, j: a("attn_D_w").T,
            "a": lambda h, j: a("attn_Wa_w")[h].T,
            "b": lambda h, j: a("attn_Wb_w")[h].T,
            "c": lambda h, j: a("attn_C_w")[h].T,
            "f1": lambda n, j: a("attn_ffn1_w")[n * P:(n + 1) * P].T,
            "f2": lambda n, j: a("attn_ffn2_w")[:, n * P:(n + 1) * P].T,
            "up": lambda e, j: (a("ffn_Wfc_s") if e == 0 else a("ffn_Wfc")[e - 1])[:, j * P:(j + 1) * P],
            "dn": lambda e, j: (a("ffn_Wproj_s") if e == 0 else a("ffn_Wproj")[e - 1])[j * P:(j + 1) * P]}
    weights = np.concatenate([mats[n](i, j) for n, i, j in BLOCKS], axis=1)
    native = np.concatenate([mats[n](i, j) for n, i, j in NATIVE] + [a("ffn_Wr")], axis=1)
    params = np.concatenate([
        a("attn_Wa_b").T, a("attn_Wb_b").T, a("attn_C_b").T, a("attn_D_b")[:, None], a("attn_hn_b").T,
        a("attn_ffn1_b").reshape(F, P).T, a("attn_ffn2_b")[:, None],
        a("ffn_bfc_s").reshape(F, P).T, a("ffn_bfc").reshape(X * F, P).T,
        a("ffn_bproj_s")[:, None], a("ffn_bproj").T], axis=1)
    rows = np.stack([a("attn_Wout_b"), a("attn_norm_g"), a("attn_norm_b"), a("attn_proj_b")])
    heads = np.tile(np.concatenate([a("attn_hn_g"), a("attn_head_w")[:, None]], axis=1), (SR // H, 1))

    consts = np.zeros((P, NCON), np.float32)
    consts[:, C_ID:C_ID + P] = np.eye(P)
    for h in range(H):
        consts[[h, H + h, 2 * H + h], C_HM + h] = 1
    for e in range(X):
        consts[[e, X + e], C_EM + e] = 1
    consts[0:2 * H, C_HI] = consts[3 * H:5 * H, C_HI] = 1
    consts[2 * H:3 * H, C_LO] = consts[5 * H:6 * H, C_LO] = 1
    consts[3 * H:6 * H, C_Q] = 1
    consts[:, C_IO:C_IO + X] = np.arange(X)

    arrays = {"emb": a("attn_emb").reshape(B * L, E), "weights": weights, "native": native, "params": params,
              "rows": rows, "heads": heads, "head_w": a("attn_head_w"), "consts": consts}
    arrays = {k: np.ascontiguousarray(v) for k, v in arrays.items()}
    nc = bacc.Bacc("TRN2", target_bir_lowering=False, num_devices=1)
    args = [nc.dram_tensor(k, v.shape, mybir.dt.from_np(v.dtype), kind="ExternalInput").ap()
            for k, v in arrays.items()]
    out = nc.dram_tensor("out", (B * L, E), mybir.dt.float32, kind="ExternalOutput").ap()
    build(nc, *args, out)
    r = run_bass_kernel_spmd(nc, [arrays], core_ids=[0])
    return r.results[0]["out"].reshape(B, L, E)
```

```python
from contextlib import ExitStack

import concourse.bass as bass
from concourse import mybir

P = 128
B, L, E = 4, 512, 128
T = L // P
H = 8
X = 8
F = 4
NE = X + 1
NH = NE * F
EPS = 1e-5

WA_B, WB_B, C_B, D_B, HN_B = 0, H, 2 * H, 3 * H, 3 * H + 1
F1_B = HN_B + H
F2_B = F1_B + F
FC_B = F2_B + 1
PR_B = FC_B + NH
NPAR = PR_B + NE

SR = 6 * H
C_ID, C_HM = 0, P
C_EM = C_HM + H
C_HI = C_EM + X
C_LO = C_HI + 1
C_Q = C_LO + 1
C_IO = C_Q + 1
NCON = C_IO + X

NATIVE_DOWN = 2


def is_split(j):
    return j < F - NATIVE_DOWN


def splits(i):
    return sum(is_split(k % F) for k in range(i + 1))


NSP = splits(NH - 1)

BLOCKS = [("d", 0, 0)] + [(n, h, 0) for h in range(H) for n in "ab"] + [("f1", j, 0) for j in range(F)]
NA = len(BLOCKS)
BLOCKS += [(n, e, j) for e in range(NE) for n in ("up", "dn") for j in range(F) if n == "up" or is_split(j)]
BLOCK_AT = {b: i for i, b in enumerate(BLOCKS)}
NATIVE = [("c", h, 0) for h in range(H)] + [("wout", 0, 0)] + [("f2", j, 0) for j in range(F)] + [("proj", 0, 0)]
NNA = len(NATIVE)
NATIVE += [("dn", e, j) for e in range(NE) for j in range(F) if not is_split(j)]
NATIVE_AT = {b: i for i, b in enumerate(NATIVE)}
GW = 4
GROUPS = [(s, min(s + GW, end)) for start, end in ((0, NA), (NA, len(BLOCKS))) for s in range(start, end, GW)]
NG = len(GROUPS)
NGA = -(-NA // GW)
NS = 18
RAW = F
LAG = 3
R = LAG + 1

HH = 2
HN = H // HH
LINKS_A1, LINKS_A2, LINKS_O = 12, 17, 3

CUT = 10


def table(places):
    order = {k: [] for k in range(NH)}
    for k, *step in places:
        order[k].append(step)
    return order


A1_ALONE = table([
    (0, 1, "x_stats"), (0, 1, "x_norm"), (1, 1, "x_turn"), (3, 1, "dx"), (3, 1, "gate_a", 0),
    (3, 1, "gate_b", 0), (4, 1, "gate_a", 1), (4, 1, "gate_b", 1), (4, 1, "out", 0), (4, 1, "gate_a", 2),
    (4, 1, "gate_b", 2), (4, 1, "out", 1), (4, 1, "turn", 0), (6, 1, "gate_a", 3), (6, 1, "gate_b", 3),
    (6, 1, "out", 2), (6, 1, "turn", 1), (7, 1, "gate_a", 4), (7, 1, "gate_b", 4), (7, 1, "out", 3),
    (7, 1, "turn", 2), (8, 1, "gate_a", 5), (8, 1, "gate_b", 5), (8, 1, "out", 4), (8, 1, "turn", 3),
    (8, 1, "out", 5), (9, 1, "gate_a", 6), (9, 1, "gate_b", 6), (9, 1, "turn", 4), (9, 1, "h_var", 0),
    (10, 1, "gate_a", 7), (10, 1, "gate_b", 7), (10, 1, "out", 6), (10, 1, "turn", 5), (11, 1, "turn", 6),
    (11, 1, "h_pack", 0), (11, 1, "out", 7), (12, 1, "acc_start"), (12, 1, "turn", 7), (13, 1, "h_var", 1),
    (14, 1, "h_pack", 1), (18, 1, "h_turn"),
])
NO_EXPERTS = table([
    (0, 2, "scale", 0), (0, 1, "x_stats"), (1, 2, "scale", 1), (1, 1, "x_norm"), (1, 2, "scale", 2),
    (2, 1, "x_turn"), (2, 2, "scale", 3), (3, 2, "scale", 4), (3, 1, "dx"), (4, 2, "scale", 5),
    (4, 1, "gate_a", 0), (5, 1, "gate_b", 0), (6, 2, "scale", 6), (7, 1, "out", 0), (7, 1, "gate_a", 1),
    (7, 2, "scale", 7), (7, 1, "turn", 0), (8, 1, "gate_b", 1), (8, 1, "gate_a", 2), (8, 1, "out", 1),
    (9, 2, "z"), (9, 1, "gate_b", 2), (9, 1, "turn", 1), (10, 1, "gate_a", 3), (10, 1, "out", 2), (11, 2, "u"),
    (11, 1, "gate_b", 3), (11, 1, "turn", 2), (11, 1, "acc_start"), (12, 2, "u_turn"), (12, 1, "gate_a", 4),
    (12, 1, "out", 3), (14, 1, "gate_b", 4), (14, 1, "turn", 3), (14, 2, "ffn_up"), (16, 1, "gate_a", 5),
    (16, 1, "out", 4), (16, 1, "h_var", 0), (16, 1, "gate_b", 5), (16, 2, "ffn_down"), (16, 2, "h_out"),
    (16, 1, "turn", 4), (17, 1, "gate_a", 6), (17, 1, "out", 5), (17, 2, "proj"), (17, 1, "turn", 5),
    (18, 1, "gate_b", 6), (18, 1, "out", 6), (19, 1, "gate_a", 7), (19, 2, "attention"), (19, 1, "gate_b", 7),
    (19, 1, "turn", 6), (20, 1, "h_pack", 0), (20, 1, "out", 7), (21, 2, "x1_norm"), (21, 1, "turn", 7),
    (21, 1, "h_var", 1), (21, 2, "x1_turn"), (22, 2, "route"), (23, 1, "h_pack", 1), (23, 2, "gate"),
    (24, 1, "h_turn"), (25, 2, "x2_split"), (28, 2, "gate_turn"),
])
ORDER = table([
    (0, 2, "scale", 0), (1, 2, "scale", 1), (1, 1, "x_stats"), (2, 2, "scale", 2), (3, 1, "x_norm"),
    (3, 2, "scale", 3), (4, 1, "x_turn"), (5, 2, "scale", 4), (5, 2, "scale", 5), (6, 1, "dx"),
    (6, 2, "scale", 6), (6, 1, "gate_a", 0), (7, 2, "scale", 7), (8, 1, "gate_b", 0), (9, 2, "z"),
    (9, 1, "gate_a", 1), (10, 1, "out", 0), (10, 2, "u"), (10, 1, "acc_start"), (11, 1, "gate_b", 1),
    (12, 1, "turn", 0), (12, 2, "u_turn"), (12, 1, "gate_a", 2), (14, 1, "out", 1), (14, 2, "ffn_up"),
    (14, 1, "gate_b", 2), (15, 2, "ffn_down"), (15, 2, "h_out"), (15, 1, "turn", 1), (15, 1, "gate_a", 3),
    (15, 2, "proj"), (16, 1, "out", 2), (18, 1, "turn", 2), (18, 1, "gate_b", 3), (18, 2, "attention"),
    (19, 1, "out", 3), (19, 1, "gate_a", 4), (19, 1, "gate_b", 4), (20, 2, "x1_norm"), (20, 1, "turn", 3),
    (20, 1, "gate_a", 5), (21, 2, "x1_turn"), (21, 1, "h_var", 0), (22, 2, "route"), (22, 1, "out", 4),
    (22, 1, "gate_b", 5), (23, 1, "turn", 4), (24, 1, "out", 5), (24, 1, "h_pack", 0), (25, 1, "gate_a", 6),
    (25, 2, "x2_split"), (25, 1, "turn", 5), (25, 1, "gate_b", 6), (25, 2, "gate"), (26, 1, "out", 6),
    (26, 1, "gate_a", 7), (27, 1, "turn", 6), (27, 1, "gate_b", 7), (29, 1, "out", 7), (30, 1, "turn", 7),
    (31, 2, "gate_turn"), (32, 1, "h_var", 1), (34, 1, "h_pack", 1), (35, 1, "h_turn"),
])
A2_LAST = table([
    (0, 2, "scale", 0), (1, 2, "scale", 1), (2, 2, "scale", 2), (3, 2, "scale", 3), (5, 2, "scale", 4),
    (5, 2, "scale", 5), (6, 2, "scale", 6), (7, 2, "scale", 7), (9, 2, "z"), (10, 2, "u"), (12, 2, "u_turn"),
    (13, 2, "ffn_up"), (15, 2, "ffn_down"), (15, 2, "h_out"), (15, 2, "proj"), (18, 2, "attention"),
    (20, 2, "x1_norm"), (22, 2, "x1_turn"), (23, 2, "route"), (25, 2, "x2_split"), (25, 2, "gate"),
    (32, 2, "gate_turn"),
])
PREV = {2: "last_y", 3: "last_gated", 4: "last_sum", 5: "y_turn", 6: "out_stats", 7: "out_norm"}
KEEP = 9


def build(nc, emb, weights, native, params, rows, heads, head_w, consts, out):
    fp32, f32r, u32 = mybir.dt.float32, mybir.dt.float32r, mybir.dt.uint32
    ALU, ACT = mybir.AluOpType, mybir.ActivationFunctionType
    AX = mybir.AxisListType.X
    ctx = ExitStack()
    with ctx:
        def sb(name, shape, dt=fp32):
            return ctx.enter_context(nc.sbuf_tensor(name, shape, dt))

        def sem(name):
            return ctx.enter_context(nc.semaphore(name))

        w_raw = sb("w_raw", [P, RAW, GW * P])
        w_hi = sb("w_hi", [P, len(BLOCKS), P], f32r)
        w_lo = sb("w_lo", [P, len(BLOCKS), P], f32r)
        w_nat = sb("w_nat", [P, len(NATIVE), P])
        w_router = sb("w_router", [P, P])
        par = sb("par", [P, NPAR])
        row = sb("row", [P, 4, P])
        con = sb("con", [P, NCON])
        hrow = sb("hrow", [P, P + 1])
        hhi = sb("hhi", [P, P], f32r)
        hsel = sb("hsel", [P, H + 1, P], f32r)
        esel = sb("esel", [P, X, P], f32r)
        hw = sb("hw", [P, H])
        hb = sb("hb", [P, H])
        dx8_b = sb("dx8_b", [P, 1])
        mhalf = sb("mhalf", [P, T * H])

        x_tok = sb("x_tok", [P, T, E])
        xn = sb("xn", [P, T, E])
        xT_hi = sb("xT_hi", [P, L], f32r)
        xT_lo = sb("xT_lo", [P, L], f32r)
        dx = sb("dx", [P, L])
        rT = sb("rT", [P, L], f32r)
        tok = sb("tok", [P, 2, T, E])
        uT_hi = sb("uT_hi", [P, L], f32r)
        uT_lo = sb("uT_lo", [P, L], f32r)
        h_res = sb("h_res", [P, L])
        hlo, hstack = h_res[:, 0:P], h_res[:, P:2 * P]
        acc = sb("acc", [P, L])
        a_t = sb("a_t", [P, L])
        b_t = sb("b_t", [P, L])
        o_t = sb("o_t", [P, H, L])
        st_i = sb("st_i", [P, T, 6])
        mv_i = sb("mv_i", [P, T, 2])
        ve_i = sb("ve_i", [P, T])
        rs_i = sb("rs_i", [P, T])
        st_a = sb("st_a", [P, T, 6])
        mv_a = sb("mv_a", [P, T, 2])
        ve_a = sb("ve_a", [P, T])
        rs_a = sb("rs_a", [P, T])
        st_h = sb("st_h", [P, T * H, 6])
        sm_h = sb("sm_h", [P, T * H])
        df_h = sb("df_h", [P, T * H])
        m2_h = sb("m2_h", [P, T * H])
        ve_h = sb("ve_h", [P, T * H])
        rs_h = sb("rs_h", [P, T * H])
        q_h = sb("q_h", [P, T * H])
        rq = sb("rq", [P, T, P])

        x1 = sb("x1", [P, T, E])
        x1_out = sb("x1_out", [P, T, E])
        tokb = sb("tokb", [P, T, E])
        res = sb("res", [P, T, E])
        x2_f = sb("x2_f", [P, L])
        x2_hi = sb("x2_hi", [P, L], f32r)
        x2_lo = sb("x2_lo", [P, L], f32r)
        y_acc = sb("y_acc", [P, L])
        y_e = sb("y_e", [P, L])
        g_t = sb("g_t", [P, R, L])
        g_hi = sb("g_hi", [P, F - NATIVE_DOWN, L], f32r)
        g_lo = sb("g_lo", [P, F - NATIVE_DOWN, L], f32r)
        st_b = sb("st_b", [P, T, 6])
        mv_b = sb("mv_b", [P, T, 2])
        ve_b = sb("ve_b", [P, T])
        rs_b = sb("rs_b", [P, T])
        lg = sb("lg", [P, T, X])
        top = sb("top", [P, T, 8])
        idx = sb("idx", [P, T, 8], u32)
        idf = sb("idf", [P, T, 8])
        gap = sb("gap", [P, T])
        th = sb("th", [P, T])
        gv = sb("gv", [P, 2, T])
        g1 = sb("g1", [P, T, X])
        g2 = sb("g2", [P, T, X])
        gate = sb("gate", [P, T, P])
        gT = sb("gT", [P, L], f32r)

        ps = [ctx.enter_context(nc.psum_tensor(f"ps{i}", [P, L], fp32)) for i in range(8)]
        p_hid, p_y, p_g = ps[0:2], ps[2], ps[3]
        p_ab, p_c, p_u, p_v = ps[4:8]

        s_raw = [sem(f"s_raw{i}") for i in range(RAW)]
        s_con, s_row, s_nat, s_natb, s_zero, s_whi, s_wlo, s_chain, s_bias, s_setup = (
            sem(n) for n in ("s_con", "s_row", "s_nat", "s_natb", "s_zero", "s_whi", "s_wlo", "s_chain", "s_bias", "s_setup"))
        x_in = sem("x_in")
        x1_in = sem("x1_in")
        va1 = sem("va1")
        va2 = sem("va2")
        var_i = sem("var_i")
        rstd_i = sem("rstd_i")
        var_a = sem("var_a")
        rstd_a = sem("rstd_a")
        var_h = sem("var_h")
        rstd_h = sem("rstd_h")
        xh = sem("xh")
        xt_mm = sem("xt_mm")
        xt_hi = sem("xt_hi")
        xt_lo = sem("xt_lo")
        dx_mm = sem("dx_mm")
        dx_sb = sem("dx_sb")
        a_mm = sem("a_mm")
        a_sb = sem("a_sb")
        b_mm = sem("b_mm")
        b_sb = sem("b_sb")
        scan = sem("scan")
        c_mm = sem("c_mm")
        o_sb = sem("o_sb")
        ot_mm = sem("ot_mm")
        o_bn = sem("o_bn")
        rq_sb = sem("rq_sb")
        rq_mm = sem("rq_mm")
        rt_sb = sem("rt_sb")
        rb_mm = sem("rb_mm")
        q_mm = sem("q_mm")
        scaled = sem("scaled")
        summed = sem("summed")
        z_mm = sem("z_mm")
        u_sb = sem("u_sb")
        ut_mm = sem("ut_mm")
        ut_sb = sem("ut_sb")
        ut_lo = sem("ut_lo")
        f_mm = sem("f_mm")
        f_sb = sem("f_sb")
        f_dn = sem("f_dn")
        ho_sb = sem("ho_sb")
        p_mm = sem("p_mm")
        att = sem("att")
        x1_sb = sem("x1_sb")
        x1_kept = sem("x1_kept")
        var_x = sem("var_x")
        rstd_x = sem("rstd_x")
        x2_tok = sem("x2_tok")
        x2_mm = sem("x2_mm")
        x2_fs = sem("x2_fs")
        x2_h = sem("x2_h")
        x2_l = sem("x2_l")
        lg_mm = sem("lg_mm")
        gap_sb = sem("gap_sb")
        th_sb = sem("th_sb")
        gate_sb = sem("gate_sb")
        gt_mm = sem("gt_mm")
        gt_sb = sem("gt_sb")
        up_mm = sem("up_mm")
        h_sb = sem("h_sb")
        h_hi = sem("h_hi")
        h_lo = sem("h_lo")
        dn_mm = sem("dn_mm")
        y_sb = sem("y_sb")
        gb_mm = sem("gb_mm")
        gated = sem("gated")
        y_sum = sem("y_sum")
        yt_mm = sem("yt_mm")
        vo = sem("vo")
        var_o = sem("var_o")
        rstd_o = sem("rstd_o")
        out_sb = sem("out_sb")
        stored = sem("stored")
        res_free = sem("res_free")

        def ident():
            return con[:, C_ID:C_ID + P]

        def col(k):
            return par[:, k:k + 1]

        def tile(t):
            return slice(t * P, (t + 1) * P)

        def wait(eng, s, value):
            if not isinstance(value, int) or value > 0:
                eng.wait_ge(s, value)

        def chunks(eng, body):
            body(None, None, None, 0)
            body(None, 0, 0, 1)
            with eng.Fori(0, B - 2) as c:
                body(c, c + 1, c + 1, c + 2)
            body(B - 2, B - 1, B - 1, None)
            body(B - 1, None, None, None)

        def run(k, c, start, a2, a1, slot, prev, steps, keep=None):
            i = (CUT + k) % NH
            fresh = CUT + k >= NH
            if c is not None or start is not None:
                slot(i, start if fresh else c, c if fresh else None)
            if fresh and c is not None and PREV.get(i) in prev:
                prev[PREV[i]](c)
            if fresh and start is not None and i == KEEP and keep:
                keep(start)
            order = A1_ALONE if a2 is None and c is None else NO_EXPERTS if c is None else A2_LAST if a1 is None else ORDER
            for stage, name, *arg in order[k]:
                chunk = (a1, a2)[stage - 1]
                if chunk is not None and name in steps:
                    steps[name](chunk, *arg)

        def is_first(c):
            return isinstance(c, int) and c == 0

        def y_bank(c, e):
            return p_c if is_late(c, e) and e % 2 else p_y

        def is_late(c, e):
            return isinstance(c, int) and (c == B - 1 or c == B - 2 and e > 2)

        def is_wide(c):
            return isinstance(c, int)

        block = ctx.enter_context(nc.Block())

        @block.sync
        def _(sp):
            def load(dst, c, done):
                sp.dma_start(dst[:, :, :],
                             emb[bass.ds(c * L, L), :].rearrange("(t p) e -> p t e", p=P)).then_inc(done, 16)

            def store(c):
                sp.wait_ge(out_sb, c + 1)
                sp.dma_start(out[bass.ds(c * L, L), :].rearrange("(t p) e -> p t e", p=P),
                             res[:, :, :]).then_inc(stored, 16)
                sp.wait_ge(stored, c * 16 + 16)
                sp.sem_inc(res_free, 1)

            load(x_tok, 0, x_in)
            sp.dma_start(con[:, :], consts).then_inc(s_con, 16)
            sp.dma_start(par[:, :], params).then_inc(s_con, 16)
            sp.dma_start(hw[:, :], head_w.partition_broadcast(P)).then_inc(s_con, 16)
            sp.sem_inc(res_free, 1)
            for g, (b0, b1) in enumerate(GROUPS):
                if g >= RAW:
                    sp.wait_ge(s_wlo, g - RAW + 1)
                sp.dma_start(w_raw[:, g % RAW, 0:(b1 - b0) * P],
                             weights[:, b0 * P:b1 * P]).then_inc(s_raw[g % RAW], 16)
                if g == RAW - 1:
                    sp.dma_start(hrow[0:SR, :], heads).then_inc(s_row, 16)
                    sp.dma_start(w_nat[:, 0:NNA, :],
                                 native[:, 0:NNA * P].rearrange("p (n e) -> p n e", e=P)).then_inc(s_nat, 16)
                    sp.dma_start(row[:, :, :], rows.partition_broadcast(P)).then_inc(s_row, 16)
                if g == NGA:
                    load(x1, 0, x1_in)
                    sp.wait_ge(xh, 1)
                    load(x_tok, 1, x_in)
                    sp.wait_ge(s_zero, 3)
                    sp.dma_start(w_router[:, 0:X],
                                 native[:, len(NATIVE) * P:len(NATIVE) * P + X]).then_inc(s_natb, 16)
                    sp.dma_start(w_nat[:, NNA:, :],
                                 native[:, NNA * P:len(NATIVE) * P].rearrange("p (n e) -> p n e", e=P)
                                 ).then_inc(s_natb, 16)
            with sp.Fori(0, B - 2) as c:
                sp.wait_ge(xh, c + 2)
                load(x_tok, c + 2, x_in)
                sp.wait_ge(x1_kept, c + 1)
                load(x1, c + 1, x1_in)
                store(c)
            sp.wait_ge(x1_kept, B - 1)
            load(x1, B - 1, x1_in)
            store(B - 2)
            store(B - 1)
            sp.wait_ge(stored, B * 16)

        @block.gpsimd
        def _(pool):
            nc.gpsimd.memset(mhalf[:, :], -0.5).then_inc(s_zero, 1)
            nc.gpsimd.memset(hstack[:, :], 0.0).then_inc(s_zero, 1)
            nc.gpsimd.memset(w_router[:, :], 0.0).then_inc(s_zero, 1)
            nc.gpsimd.memset(rq[:, :, :], 0.0).then_inc(s_zero, 1)
            nc.gpsimd.memset(gate[:, :, :], 0.0).then_inc(s_zero, 1)
            pool.wait_ge(s_zero, 5)

            def rstd(out_, var, var_ready, n, done):
                pool.wait_ge(var_ready, n)
                nc.gpsimd.tensor_tensor(out=out_, in0=var, in1=mhalf[:, 0:out_.shape[1]],
                                        op=ALU.pow).then_inc(done, 1)

            def x_stats(c):
                rstd(rs_i[:, :], ve_i[:, :], var_i, c + 1, rstd_i)

            def h_var(c, k):
                half = slice(k * T * HN, (k + 1) * T * HN)
                rstd(rs_h[:, half], ve_h[:, half], var_h, c * HH + k + 1, rstd_h)

            def z(c):
                rstd(rs_a[:, :], ve_a[:, :], var_a, c * 2 + 1, rstd_a)

            def proj(c):
                rstd(rs_a[:, :], ve_a[:, :], var_a, c * 2 + 2, rstd_a)

            def attention(c):
                rstd(rs_b[:, :], ve_b[:, :], var_x, c + 1, rstd_x)

            def out_stats(c):
                rstd(rs_b[:, :], ve_b[:, :], var_o, c + 1, rstd_o)

            def keep(c):
                pool.wait_ge(x1_sb, c + 1)
                wait(pool, out_sb, c)
                nc.gpsimd.nop(nofuse=True)
                nc.gpsimd.tensor_copy(x1_out[:, :, :], x1[:, :, :]).then_inc(x1_kept, 1)

            STEPS = {"x_stats": x_stats, "h_var": h_var, "z": z, "proj": proj, "attention": attention}

            def body(c, start, a2, a1):
                for k in range(NH):
                    run(k, c, start, a2, a1, lambda i, own, before: None, {"out_stats": out_stats}, STEPS, keep)

            chunks(pool, body)

        @block.tensor
        def _(pe):
            def mm3(dst, name, x_hi, x_lo, start=True, stop=True):
                w = BLOCK_AT[name]
                nc.tensor.matmul(dst, w_hi[:, w, :], x_hi, start=start, stop=False)
                nc.tensor.matmul(dst, w_lo[:, w, :], x_hi, start=False, stop=False)
                return nc.tensor.matmul(dst, w_hi[:, w, :], x_lo, start=False, stop=stop)

            def transposes(dst, src):
                for t in range(T):
                    last = nc.tensor.transpose(dst[:, tile(t)], src(t), ident())
                return last

            def x_turn(c):
                pe.wait_ge(xh, c + 1)
                transposes(p_ab, lambda t: xn[:, t, :]).then_inc(xt_mm, 1)

            def dx_product(c):
                pe.wait_ge(xt_lo, c + 1)
                if is_first(c):
                    pe.wait_ge(s_wlo, 1)
                mm3(p_c[:, :], ("d", 0, 0), xT_hi[:, :], xT_lo[:, :]).then_inc(dx_mm, 1)

            def gate_a(c, h):
                if is_first(c):
                    pe.wait_ge(s_wlo, BLOCK_AT["b", h, 0] // GW + 1)
                if is_wide(c):
                    wait(pe, a_sb, c * H + h)
                elif h > 0:
                    pe.wait_ge(b_sb, c * H + h)
                dst = p_hid[0] if is_wide(c) else p_ab
                mm3(dst[:, :], ("a", h, 0), xT_hi[:, :], xT_lo[:, :]).then_inc(a_mm, 1)

            def gate_b(c, h):
                if is_wide(c):
                    wait(pe, b_sb, c * H + h)
                else:
                    pe.wait_ge(a_sb, c * H + h + 1)
                dst = p_hid[1] if is_wide(c) else p_ab
                mm3(dst[:, :], ("b", h, 0), xT_hi[:, :], xT_lo[:, :]).then_inc(b_mm, 1)

            def head_out(c, h):
                pe.wait_ge(scan, c * H + h + 1)
                if h == 0:
                    pe.wait_ge(dx_sb, c + 1)
                    if is_first(c):
                        pe.wait_ge(s_nat, 16)
                elif is_wide(c):
                    pe.wait_ge(o_sb, c * H + h)
                else:
                    pe.wait_ge(o_bn, c * H + h)
                nc.tensor.matmul(p_c[:, :], w_nat[:, NATIVE_AT["c", h, 0], :], o_t[:, h, :],
                                 start=True, stop=True).then_inc(c_mm, 1)

            def turn(c, h):
                pe.wait_ge(o_sb, c * H + h + 1)
                if is_wide(c):
                    wait(pe, o_bn, c * H + h)
                transposes(p_y if is_wide(c) else p_c, lambda t: o_t[:, h, tile(t)]).then_inc(ot_mm, 1)

            def h_turn(c):
                pe.wait_ge(rq_sb, c * HH + HH)
                transposes(p_c, lambda t: rq[:, t, :]).then_inc(rq_mm, 1)

            def scale(c, h):
                if h == 0:
                    pe.wait_ge(rt_sb, c + 1)
                    wait(pe, gt_sb, c)
                    if is_first(c):
                        pe.wait_ge(s_setup, 1)
                    nc.tensor.matmul(p_u[:, :], hsel[:, H, :], rT[:, :], start=True, stop=True).then_inc(q_mm, 1)
                elif h == 1:
                    pe.wait_ge(summed, c * (H + 1) + 1)
                else:
                    pe.wait_ge(scaled, c * H + h - 1)
                nc.tensor.matmul((p_v, p_u)[h % 2][:, :], hsel[:, h, :], rT[:, :],
                                 start=True, stop=True).then_inc(rb_mm, 1)

            def z(c):
                pe.wait_ge(summed, c * (H + 1) + H + 1)
                for t in range(T):
                    last = nc.tensor.matmul(p_u[:, tile(t)], acc[:, tile(t)], w_nat[:, NATIVE_AT["wout", 0, 0], :],
                                            start=True, stop=True)
                last.then_inc(z_mm, 1)

            def u_turn(c):
                pe.wait_ge(u_sb, c + 1)
                transposes(p_v, lambda t: tok[:, 1, t, :]).then_inc(ut_mm, 1)

            def ffn_up(c):
                pe.wait_ge(ut_lo, c + 1)
                if is_first(c):
                    pe.wait_ge(s_wlo, NG)
                for j in range(F):
                    if j >= 2:
                        pe.wait_ge(f_sb, c * F + j - 1)
                    mm3((p_u, p_v)[j % 2][:, :], ("f1", j, 0), uT_hi[:, :], uT_lo[:, :]).then_inc(f_mm, 1)

            def ffn_down(c):
                pe.wait_ge(f_sb, c * F + 3)
                for j in range(F):
                    if j == 3:
                        pe.wait_ge(f_sb, c * F + j + 1)
                    ins = nc.tensor.matmul(p_u[:, :], w_nat[:, NATIVE_AT["f2", j, 0], :], w_raw[:, j, :],
                                           start=(j == 0), stop=(j == F - 1))
                ins.then_inc(f_dn, 1)

            def proj(c):
                pe.wait_ge(ho_sb, c + 1)
                for t in range(T):
                    last = nc.tensor.matmul(p_v[:, tile(t)], h_res[:, tile(t)], w_nat[:, NATIVE_AT["proj", 0, 0], :],
                                            start=True, stop=True)
                last.then_inc(p_mm, 1)

            def x1_turn(c):
                pe.wait_ge(x2_tok, c + 1)
                transposes(p_u, lambda t: tokb[:, t, :]).then_inc(x2_mm, 1)

            def route(c):
                pe.wait_ge(x2_fs, c + 1)
                if is_first(c):
                    pe.wait_ge(s_natb, 32)
                for t in range(T):
                    last = nc.tensor.matmul(p_v[:, tile(t)], x2_f[:, tile(t)], w_router[:, :], start=True, stop=True)
                last.then_inc(lg_mm, 1)

            def gate_turn(c):
                pe.wait_ge(gate_sb, c + 1)
                transposes(p_u, lambda t: gate[:, t, :]).then_inc(gt_mm, 1)

            STEPS = {"x_turn": x_turn, "dx": dx_product, "gate_a": gate_a, "gate_b": gate_b, "out": head_out, "turn": turn,
                     "h_turn": h_turn, "scale": scale, "z": z, "u_turn": u_turn, "ffn_up": ffn_up,
                     "ffn_down": ffn_down, "proj": proj, "x1_turn": x1_turn, "route": route, "gate_turn": gate_turn}

            def b_up(c, i):
                if i == 0:
                    pe.wait_ge(x2_l, c + 1)
                if i >= 2 or not is_first(c):
                    pe.wait_ge(h_sb, c * NH + i - 1)
                mm3(p_hid[i % 2][:, :], ("up", i // F, i % F), x2_hi[:, :], x2_lo[:, :]).then_inc(up_mm, 1)

            def b_gate_bc(c, e):
                if e == 1:
                    pe.wait_ge(gt_sb, c + 1)
                    wait(pe, out_sb, c)
                else:
                    pe.wait_ge(gated, c * X + e - 1)
                nc.tensor.matmul(p_g[:, :], esel[:, e - 1, :], gT[:, :], start=True, stop=True).then_inc(gb_mm, 1)

            def b_down(c, i):
                e, j = i // F, i % F
                if j == 0:
                    wait(pe, y_sb, c * NE + e - (1 if e > 0 and is_late(c, e) else 0))
                first, last = j == 0, j == F - 1
                if is_split(j):
                    pe.wait_ge(h_lo, c * NSP + splits(i))
                    ins = mm3(y_bank(c, e)[:, :], ("dn", e, j), g_hi[:, j, :], g_lo[:, j, :], start=first, stop=last)
                else:
                    pe.wait_ge(h_sb, c * NH + i + 1)
                    ins = nc.tensor.matmul(y_bank(c, e)[:, :], w_nat[:, NATIVE_AT["dn", e, j], :], g_t[:, i % R, :],
                                           start=first, stop=last)
                ins.then_inc(dn_mm, 1)

            def y_turn(c):
                pe.wait_ge(y_sum, c * X + X)
                transposes(p_g, lambda t: y_acc[:, tile(t)]).then_inc(yt_mm, 1)

            def slot(i, own, before):
                if own is not None:
                    b_up(own, i)
                d, c = (i - LAG, own) if i >= LAG else (i - LAG + NH, before)
                if c is not None:
                    b_down(c, d)
                    if d % F == 2 and d >= F:
                        b_gate_bc(c, d // F)

            def body(c, start, a2, a1):
                for k in range(NH):
                    run(k, c, start, a2, a1, slot, {"y_turn": y_turn}, STEPS)

            pe.wait_ge(s_con, 3 * 16)
            pe.wait_ge(s_zero, 5)
            chunks(pe, body)

        @block.scalar
        def _(act):
            def copy(dst, src):
                return nc.scalar.activation(dst, src, ACT.Copy)

            def split_weights(k, alone):
                g = k if alone else NS + k
                if g >= (NS if alone else NG):
                    return
                b0, b1 = GROUPS[g]
                act.wait_ge(s_raw[g % RAW], 16 * (g // RAW + 1))
                copy(w_hi[:, b0:b1, :], w_raw[:, g % RAW, 0:(b1 - b0) * P]
                     .rearrange("p (b n) -> p b n", n=P)).then_inc(s_whi, 1)

            def x_turn(c):
                act.wait_ge(xt_mm, c + 1)
                copy(xT_hi[:, :], p_ab[:, :]).then_inc(xt_hi, 1)

            def dx_start(c):
                act.wait_ge(dx_mm, c + 1)
                nc.scalar.activation(dx[:, :], p_c[:, :], ACT.Identity, bias=col(D_B)).then_inc(dx_sb, 1)

            def gate_a(c, h):
                act.wait_ge(a_mm, c * H + h + 1)
                if h >= 1:
                    act.wait_ge(scan, c * H + h)
                src = p_hid[0] if is_wide(c) else p_ab
                nc.scalar.activation(a_t[:, :], src[:, :], ACT.Tanh, bias=col(WA_B + h)).then_inc(a_sb, 1)

            def gate_b(c, h):
                act.wait_ge(b_mm, c * H + h + 1)
                src = p_hid[1] if is_wide(c) else p_ab
                nc.scalar.activation(b_t[:, :], src[:, :], ACT.Identity, bias=col(WB_B + h)).then_inc(b_sb, 1)

            def acc_start(c):
                act.wait_ge(dx_sb, c + 1)
                wait(act, z_mm, c)
                if is_first(c):
                    act.wait_ge(s_bias, 1)
                nc.scalar.activation(acc[:, :], dx[:, :], ACT.Identity, bias=dx8_b[:, :], scale=1.0 / H)

            def h_turn(c):
                act.wait_ge(rq_mm, c + 1)
                copy(rT[:, :], p_c[:, :]).then_inc(rt_sb, 1)

            def u_turn(c):
                act.wait_ge(ut_mm, c + 1)
                copy(uT_hi[:, :], p_v[:, :])
                nc.scalar.activation(h_res[:, :], p_v[:, :], ACT.Identity, bias=col(F2_B)).then_inc(ut_sb, 1)

            def ffn_up(c):
                for j in range(F):
                    act.wait_ge(f_mm, c * F + j + 1)
                    nc.scalar.activation(w_raw[:, j, :], (p_u, p_v)[j % 2][:, :], ACT.Gelu,
                                         bias=col(F1_B + j)).then_inc(f_sb, 1)

            def x1_turn(c):
                act.wait_ge(x2_mm, c + 1)
                copy(x2_f[:, :], p_u[:, :]).then_inc(x2_fs, 1)

            def x2_split(c):
                act.wait_ge(x2_fs, c + 1)
                wait(act, up_mm, c * NH)
                copy(x2_hi[:, :], x2_f[:, :]).then_inc(x2_h, 1)

            def gate(c):
                act.wait_ge(gap_sb, c + 1)
                nc.scalar.activation(th[:, :], gap[:, :], ACT.Tanh, scale=0.5).then_inc(th_sb, 1)

            def gate_turn(c):
                act.wait_ge(gt_mm, c + 1)
                copy(gT[:, :], p_u[:, :]).then_inc(gt_sb, 1)

            STEPS = {"x_turn": x_turn, "dx": dx_start, "gate_a": gate_a, "gate_b": gate_b, "acc_start": acc_start,
                     "x2_split": x2_split, "h_turn": h_turn, "u_turn": u_turn,
                     "ffn_up": ffn_up, "x1_turn": x1_turn, "gate": gate, "gate_turn": gate_turn}

            def b_gelu(c, i):
                act.wait_ge(up_mm, c * NH + i + 1)
                nc.scalar.activation(g_t[:, i % R, :], p_hid[i % 2][:, :], ACT.Gelu_apprx_tanh,
                                     bias=col(FC_B + i)).then_inc(h_sb, 1)

            def b_hi(c, i):
                act.wait_ge(h_sb, c * NH + i + 1)
                copy(g_hi[:, i % F, :], g_t[:, i % R, :]).then_inc(h_hi, 1)

            def b_y(c, e):
                act.wait_ge(dn_mm, c * NH + e * F + F)
                if e == 0:
                    wait(act, yt_mm, c)
                elif e >= 2:
                    act.wait_ge(y_sum, c * X + e - 1)
                nc.scalar.activation((y_e if e else y_acc)[:, :], y_bank(c, e)[:, :], ACT.Identity,
                                     bias=col(PR_B + e)).then_inc(y_sb, 1)

            def last_y(c):
                b_y(c, X)

            def slot(i, c, before):
                if c is None:
                    return
                b_gelu(c, i)
                if is_split(i % F):
                    b_hi(c, i)
                if i % F == 2 and i > F:
                    b_y(c, i // F - 1)

            def body(c, start, a2, a1):
                for k in range(NH):
                    run(k, c, start, a2, a1, slot, {"last_y": last_y}, STEPS)
                    if c is None:
                        split_weights(k, a2 is None)

            act.wait_ge(s_con, 3 * 16)
            chunks(act, body)

        @block.vector
        def _(dve):
            def f(ap):
                return ap.bitcast(fp32)

            class Chain:

                def __init__(self, s, links):
                    self.s, self.links, self.k = s, links, 0

                def link(self, c, ins):
                    self.k += 1
                    ins.then_inc(self.s, 1)
                    dve.wait_ge(self.s, c * self.links + self.k)

                def end(self):
                    assert self.k == self.links, (self.k, self.links)
                    self.k = 0

            ch1, ch2, cho = Chain(va1, LINKS_A1), Chain(va2, LINKS_A2), Chain(vo, LINKS_O)

            def v_tt(dst, a, b, op):
                return nc.vector.tensor_tensor(out=dst, in0=a, in1=b, op=op)

            def v_ts(dst, a, s1, s2, op0, op1):
                return nc.vector.tensor_scalar(out=dst, in0=a, scalar1=s1, scalar2=s2, op0=op0, op1=op1)

            def split_weights(k, alone):
                g = k if alone else NS + k
                if g >= (NS if alone else NG):
                    return
                b0, b1 = GROUPS[g]
                dve.wait_ge(s_whi, g + 1)
                v_tt(w_lo[:, b0:b1, :], w_raw[:, g % RAW, 0:(b1 - b0) * P].rearrange("p (b n) -> p b n", n=P),
                     f(w_hi[:, b0:b1, :]), ALU.subtract).then_inc(s_wlo, 1)

            setup = [0]

            def link(ins):
                setup[0] += 1
                ins.then_inc(s_chain, 1)
                dve.wait_ge(s_chain, setup[0])

            def head_bias():
                dve.wait_ge(s_con, 3 * 16)
                link(v_tt(hb[:, :], par[:, HN_B:HN_B + H], hw[:, :], ALU.mult))
                link(nc.vector.reduce_sum(dx8_b[:, :], hb[:, :], axis=AX))
                v_ts(dx8_b[:, :], dx8_b[:, :], 1.0 / H, None, ALU.mult, ALU.bypass).then_inc(s_bias, 1)

            def selectors():
                dve.wait_ge(s_row, 2 * 16)
                dve.wait_ge(s_zero, 5)
                link(v_ts(hrow[0:SR, 0:P], hrow[0:SR, 0:P], hrow[0:SR, P:P + 1], 1.0 / H, ALU.mult, ALU.mult))
                link(nc.vector.tensor_copy(hhi[0:SR, :], hrow[0:SR, 0:P]))
                link(v_tt(hlo[0:SR, :], hrow[0:SR, 0:P], f(hhi[0:SR, :]), ALU.subtract))
                link(v_ts(hlo[0:SR, :], hlo[0:SR, :], con[0:SR, C_LO:C_LO + 1], None, ALU.mult, ALU.bypass))
                link(nc.vector.scalar_tensor_tensor(out=hstack[0:SR, :], in0=f(hhi[0:SR, :]),
                                                    scalar=con[0:SR, C_HI:C_HI + 1], in1=hlo[0:SR, :],
                                                    op0=ALU.mult, op1=ALU.add))
                for h in range(H):
                    v_ts(hsel[:, h, :], hstack[:, :], con[:, C_HM + h:C_HM + h + 1], None, ALU.mult, ALU.bypass)
                v_ts(hsel[:, H, :], hstack[:, :], con[:, C_Q:C_Q + 1], None, ALU.mult, ALU.bypass)
                nc.vector.tensor_copy(esel[:, :, :],
                                      con[:, C_EM:C_EM + X].unsqueeze(2).to_broadcast([P, X, P])).then_inc(s_setup, 1)

            def stats(c, chain, src, st, mv, ve, ready):
                for t in range(T):
                    ins = nc.vector.bn_stats(out=st[:, t, :], in_=src(t))
                chain.link(c, ins)
                nc.vector.nop(nofuse=True)
                for t in range(T):
                    ins = nc.vector.bn_aggr(out=mv[:, t, :], in_=st[:, t, :])
                chain.link(c, ins)
                nc.vector.tensor_scalar_add(ve[:, :], mv[:, :, 1], EPS).then_inc(ready, 1)

            def normalise(dst, src, mv, rs):
                for t in range(T):
                    ins = v_ts(dst(t), src(t), mv[:, t, 0:1], rs[:, t:t + 1], ALU.subtract, ALU.mult)
                return ins

            def spread(r):
                return row[:, r:r + 1, :].to_broadcast([P, T, P])

            def x_stats(c):
                dve.wait_ge(x_in, c * 16 + 16)
                stats(c, ch1, lambda t: x_tok[:, t, :], st_i, mv_i, ve_i, var_i)

            def x_norm(c):
                dve.wait_ge(rstd_i, c + 1)
                normalise(lambda t: xn[:, t, :], lambda t: x_tok[:, t, :], mv_i, rs_i).then_inc(xh, 1)

            def x_turn(c):
                dve.wait_ge(xt_hi, c + 1)
                v_tt(xT_lo[:, :], p_ab[:, :], f(xT_hi[:, :]), ALU.subtract).then_inc(xt_lo, 1)

            def gate_b(c, h):
                dve.wait_ge(b_sb, c * H + h + 1)
                if not is_first(c):
                    dve.wait_ge(summed, (c - 1) * (H + 1) + h + 2)
                nc.vector.tensor_tensor_scan(out=o_t[:, h, :], data0=a_t[:, :], data1=b_t[:, :],
                                             initial=0.0, op0=ALU.mult, op1=ALU.add).then_inc(scan, 1)

            def head_out(c, h):
                dve.wait_ge(c_mm, c * H + h + 1)
                nc.vector.scalar_tensor_tensor(out=o_t[:, h, :], in0=p_c[:, :], scalar=col(C_B + h), in1=dx[:, :],
                                               op0=ALU.add, op1=ALU.mult).then_inc(o_sb, 1)

            def turn(c, h):
                dve.wait_ge(ot_mm, c * H + h + 1)
                src = p_y if is_wide(c) else p_c
                for t in range(T):
                    ins = nc.vector.bn_stats(out=st_h[:, (h // HN * T + t) * HN + h % HN, :], in_=src[:, tile(t)])
                ins.then_inc(o_bn, 1)

            def h_var(c, k):
                half = slice(k * T * HN, (k + 1) * T * HN)
                dve.wait_ge(o_bn, c * H + (k + 1) * HN)
                me, m2e, mo, m2o = (st_h[:, half, n] for n in (1, 2, 4, 5))
                v_tt(df_h[:, half], me, mo, ALU.subtract)
                v_tt(sm_h[:, half], me, mo, ALU.add)
                ch1.link(c, v_tt(m2_h[:, half], m2e, m2o, ALU.add))
                ch1.link(c, v_tt(df_h[:, half], df_h[:, half], df_h[:, half], ALU.mult))
                ch1.link(c, v_ts(df_h[:, half], df_h[:, half], 0.25, EPS, ALU.mult, ALU.add))
                nc.vector.scalar_tensor_tensor(out=ve_h[:, half], in0=m2_h[:, half], scalar=1.0 / P,
                                               in1=df_h[:, half], op0=ALU.mult, op1=ALU.add).then_inc(var_h, 1)

            def h_pack(c, k):
                half = slice(k * T * HN, (k + 1) * T * HN)
                dve.wait_ge(rstd_h, c * HH + k + 1)
                r = rs_h[:, half].rearrange("p (t h) -> p t h", h=HN)
                q = q_h[:, half].rearrange("p (t h) -> p t h", h=HN)

                def part(n):
                    return rq[:, :, n * H + k * HN:n * H + (k + 1) * HN]

                nc.vector.tensor_copy(part(0).bitcast(f32r), r)
                nc.vector.tensor_copy(part(2).bitcast(f32r), r)
                ch1.link(c, nc.vector.scalar_tensor_tensor(out=q_h[:, half], in0=sm_h[:, half], scalar=-0.5,
                                                          in1=rs_h[:, half], op0=ALU.mult, op1=ALU.mult))
                v_tt(part(1), r, part(0), ALU.subtract)
                nc.vector.tensor_copy(part(5).bitcast(f32r), q)
                ch1.link(c, nc.vector.tensor_copy(part(3).bitcast(f32r), q))
                v_tt(part(4), q, part(3), ALU.subtract).then_inc(rq_sb, 1)

            def scale(c, h):
                if h == 0:
                    dve.wait_ge(q_mm, c + 1)
                    v_tt(acc[:, :], acc[:, :], p_u[:, :], ALU.add).then_inc(summed, 1)
                dve.wait_ge(rb_mm, c * H + h + 1)
                v_tt(o_t[:, h, :], o_t[:, h, :], (p_v, p_u)[h % 2][:, :], ALU.mult).then_inc(scaled, 1)
                if h >= 1:
                    add_head(c, h - 1)
                if h == H - 1:
                    add_head(c, h)

            def add_head(c, h):
                dve.wait_ge(scaled, c * H + h + 1)
                dve.wait_ge(summed, c * (H + 1) + h + 1)
                v_tt(acc[:, :], acc[:, :], o_t[:, h, :], ALU.add).then_inc(summed, 1)

            def z(c):
                dve.wait_ge(z_mm, c + 1)
                ch2.link(c, v_tt(tok[:, 0, :, :], p_u[:, :].rearrange("p (t e) -> p t e", e=E), spread(0), ALU.add))
                stats(c, ch2, lambda t: tok[:, 0, t, :], st_a, mv_a, ve_a, var_a)
                ch2.link(c, v_tt(tok[:, 1, :, :], tok[:, 0, :, :], spread(2), ALU.add))
                for t in range(T):
                    ins = nc.vector.scalar_tensor_tensor(out=tok[:, 0, t, :], in0=tok[:, 0, t, :],
                                                         scalar=mv_a[:, t, 0:1], in1=row[:, 1, :],
                                                         op0=ALU.subtract, op1=ALU.mult)
                ch2.link(c, ins)

            def u(c):
                dve.wait_ge(rstd_a, c * 2 + 1)
                for t in range(T):
                    ins = nc.vector.scalar_tensor_tensor(out=tok[:, 1, t, :], in0=tok[:, 0, t, :],
                                                         scalar=rs_a[:, t:t + 1], in1=tok[:, 1, t, :],
                                                         op0=ALU.mult, op1=ALU.add)
                ins.then_inc(u_sb, 1)

            def u_turn(c):
                dve.wait_ge(ut_sb, c + 1)
                v_tt(uT_lo[:, :], p_v[:, :], f(uT_hi[:, :]), ALU.subtract).then_inc(ut_lo, 1)

            def h_out(c):
                dve.wait_ge(f_dn, c + 1)
                v_tt(h_res[:, :], h_res[:, :], p_u[:, :], ALU.add).then_inc(ho_sb, 1)

            def proj(c):
                dve.wait_ge(p_mm, c + 1)
                ch2.link(c, v_tt(tok[:, 0, :, :], p_v[:, :].rearrange("p (t e) -> p t e", e=E), spread(3), ALU.add))
                stats(c, ch2, lambda t: tok[:, 0, t, :], st_a, mv_a, ve_a, var_a)

            def attention(c):
                dve.wait_ge(rstd_a, c * 2 + 2)
                normalise(lambda t: tok[:, 0, t, :], lambda t: tok[:, 0, t, :], mv_a, rs_a).then_inc(att, 1)
                dve.wait_ge(att, c + 1)
                dve.wait_ge(x1_in, c * 16 + 16)
                v_tt(x1[:, :, :], x1[:, :, :], tok[:, 0, :, :], ALU.add).then_inc(x1_sb, 1)
                dve.wait_ge(x1_sb, c + 1)
                stats(c, ch2, lambda t: x1[:, t, :], st_b, mv_b, ve_b, var_x)

            def x1_norm(c):
                dve.wait_ge(rstd_x, c + 1)
                normalise(lambda t: tokb[:, t, :], lambda t: x1[:, t, :], mv_b, rs_b).then_inc(x2_tok, 1)

            def x2_split(c):
                dve.wait_ge(x2_h, c + 1)
                v_tt(x2_lo[:, :], x2_f[:, :], f(x2_hi[:, :]), ALU.subtract).then_inc(x2_l, 1)

            def route(c):
                dve.wait_ge(lg_mm, c + 1)
                ch2.link(c, nc.vector.tensor_copy(lg[:, :, :], p_v[:, :].rearrange("p (t n) -> p t n", n=P)[:, :, 0:X]))
                nc.vector.nop(nofuse=True)
                for t in range(T):
                    ins = nc.vector.max(out=top[:, t, :], in_=lg[:, t, :])
                ch2.link(c, ins)
                v_tt(gap[:, :], top[:, :, 0], top[:, :, 1], ALU.subtract).then_inc(gap_sb, 1)
                for t in range(T):
                    ins = nc.vector.max_index(out=idx[:, t, :], in_max=top[:, t, :], in_values=lg[:, t, :])
                ch2.link(c, ins)
                nc.vector.tensor_copy(idf[:, :, :], idx[:, :, :])

            def gates_of_tokens(c):
                dve.wait_ge(th_sb, c + 1)
                v_ts(gv[:, 0, :], th[:, :], 0.5, 0.5, ALU.mult, ALU.add)
                ch2.link(c, v_ts(gv[:, 1, :], th[:, :], -0.5, 0.5, ALU.mult, ALU.add))
                for t in range(T):
                    v_ts(g1[:, t, :], con[:, C_IO:C_IO + X], idf[:, t, 0:1], gv[:, 0, t:t + 1], ALU.is_equal, ALU.mult)
                    ins = v_ts(g2[:, t, :], con[:, C_IO:C_IO + X], idf[:, t, 1:2], gv[:, 1, t:t + 1],
                               ALU.is_equal, ALU.mult)
                ch2.link(c, ins)
                ch2.link(c, v_tt(g1[:, :, :], g1[:, :, :], g2[:, :, :], ALU.add))
                ch2.link(c, nc.vector.tensor_copy(gate[:, :, 0:X].bitcast(f32r), g1[:, :, :]))
                v_tt(gate[:, :, X:2 * X], g1[:, :, :], gate[:, :, 0:X], ALU.subtract).then_inc(gate_sb, 1)

            STEPS = {"x_stats": x_stats, "x_norm": x_norm, "x_turn": x_turn, "gate_b": gate_b, "out": head_out,
                     "turn": turn, "h_var": h_var, "h_pack": h_pack, "scale": scale, "z": z, "u": u,
                     "u_turn": u_turn, "h_out": h_out, "proj": proj, "attention": attention, "x1_norm": x1_norm,
                     "x2_split": x2_split, "route": route, "gate": gates_of_tokens}

            def b_lo(c, i):
                dve.wait_ge(h_hi, c * NSP + splits(i))
                v_tt(g_lo[:, i % F, :], g_t[:, i % R, :], f(g_hi[:, i % F, :]), ALU.subtract).then_inc(h_lo, 1)

            def b_gated(c, e):
                dve.wait_ge(y_sb, c * NE + e + 1)
                dve.wait_ge(gb_mm, c * X + e)
                v_tt(y_e[:, :], y_e[:, :], p_g[:, :], ALU.mult).then_inc(gated, 1)

            def b_sum(c, e):
                dve.wait_ge(gated, c * X + e)
                if e >= 2:
                    dve.wait_ge(y_sum, c * X + e - 1)
                v_tt(y_acc[:, :], y_acc[:, :], y_e[:, :], ALU.add).then_inc(y_sum, 1)

            def last_gated(c):
                b_gated(c, X)

            def last_sum(c):
                b_sum(c, X)

            def out_stats(c):
                dve.wait_ge(yt_mm, c + 1)
                stats(c, cho, lambda t: p_g[:, tile(t)], st_b, mv_b, ve_b, var_o)

            def out_norm(c):
                dve.wait_ge(rstd_o, c + 1)
                dve.wait_ge(res_free, c + 1)
                cho.link(c, normalise(lambda t: res[:, t, :], lambda t: p_g[:, tile(t)], mv_b, rs_b))
                dve.wait_ge(x1_kept, c + 1)
                v_tt(res[:, :, :], res[:, :, :], x1_out[:, :, :], ALU.add).then_inc(out_sb, 1)
                cho.end()

            PREV_STEPS = {"last_gated": last_gated, "last_sum": last_sum, "out_stats": out_stats, "out_norm": out_norm}

            def slot(i, c, before):
                if c is None:
                    return
                if i >= 1 and is_split((i - 1) % F):
                    b_lo(c, i - 1)
                if i // F >= 2 and i % F == 3:
                    b_gated(c, i // F - 1)
                    b_sum(c, i // F - 1)

            def body(c, start, a2, a1):
                for k in range(NH):
                    run(k, c, start, a2, a1, slot, PREV_STEPS, STEPS)
                    if c is None:
                        split_weights(k, a2 is None)
                    if c is None and a2 is None and k == 0:
                        head_bias()
                    if c is None and a2 is None and k == H:
                        selectors()
                if a1 is not None:
                    ch1.end()
                if a2 is not None:
                    ch2.end()

            chunks(dve, body)


def kernel(**inputs):
    import numpy as np
    import concourse.bacc as bacc
    from concourse.bass_utils import run_bass_kernel_spmd

    def a(name):
        return np.asarray(inputs["L0_" + name])

    mats = {"wout": lambda n, j: a("attn_Wout_w").T,
            "proj": lambda n, j: a("attn_proj_w").T,
            "d": lambda h, j: a("attn_D_w").T,
            "a": lambda h, j: a("attn_Wa_w")[h].T,
            "b": lambda h, j: a("attn_Wb_w")[h].T,
            "c": lambda h, j: a("attn_C_w")[h].T,
            "f1": lambda n, j: a("attn_ffn1_w")[n * P:(n + 1) * P].T,
            "f2": lambda n, j: a("attn_ffn2_w")[:, n * P:(n + 1) * P].T,
            "up": lambda e, j: (a("ffn_Wfc_s") if e == 0 else a("ffn_Wfc")[e - 1])[:, j * P:(j + 1) * P],
            "dn": lambda e, j: (a("ffn_Wproj_s") if e == 0 else a("ffn_Wproj")[e - 1])[j * P:(j + 1) * P]}
    weights = np.concatenate([mats[n](i, j) for n, i, j in BLOCKS], axis=1)
    native = np.concatenate([mats[n](i, j) for n, i, j in NATIVE] + [a("ffn_Wr")], axis=1)
    params = np.concatenate([
        a("attn_Wa_b").T, a("attn_Wb_b").T, a("attn_C_b").T, a("attn_D_b")[:, None], a("attn_hn_b").T,
        a("attn_ffn1_b").reshape(F, P).T, a("attn_ffn2_b")[:, None],
        a("ffn_bfc_s").reshape(F, P).T, a("ffn_bfc").reshape(X * F, P).T,
        a("ffn_bproj_s")[:, None], a("ffn_bproj").T], axis=1)
    rows = np.stack([a("attn_Wout_b"), a("attn_norm_g"), a("attn_norm_b"), a("attn_proj_b")])
    heads = np.tile(np.concatenate([a("attn_hn_g"), a("attn_head_w")[:, None]], axis=1), (SR // H, 1))

    consts = np.zeros((P, NCON), np.float32)
    consts[:, C_ID:C_ID + P] = np.eye(P)
    for h in range(H):
        consts[[h, H + h, 2 * H + h], C_HM + h] = 1
    for e in range(X):
        consts[[e, X + e], C_EM + e] = 1
    consts[0:2 * H, C_HI] = consts[3 * H:5 * H, C_HI] = 1
    consts[2 * H:3 * H, C_LO] = consts[5 * H:6 * H, C_LO] = 1
    consts[3 * H:6 * H, C_Q] = 1
    consts[:, C_IO:C_IO + X] = np.arange(X)

    arrays = {"emb": a("attn_emb").reshape(B * L, E), "weights": weights, "native": native, "params": params,
              "rows": rows, "heads": heads, "head_w": a("attn_head_w"), "consts": consts}
    arrays = {k: np.ascontiguousarray(v) for k, v in arrays.items()}
    nc = bacc.Bacc("TRN2", target_bir_lowering=False, num_devices=1)
    args = [nc.dram_tensor(k, v.shape, mybir.dt.from_np(v.dtype), kind="ExternalInput").ap()
            for k, v in arrays.items()]
    out = nc.dram_tensor("out", (B * L, E), mybir.dt.float32, kind="ExternalOutput").ap()
    build(nc, *args, out)
    r = run_bass_kernel_spmd(nc, [arrays], core_ids=[0])
    return r.results[0]["out"].reshape(B, L, E)
```
